# Optimizing a Trainium2 kernel written in Bass

```python
import numpy as np
import jax
import jax.numpy as jnp

def _softmax(x, axis=-1):
    return jax.nn.softmax(x, axis=axis)

def _gelu(x):
    return jax.nn.gelu(x, approximate=True)

def _silu(x):
    return jax.nn.silu(x)

def _sigmoid(x):
    return jax.nn.sigmoid(x)

def _layernorm(x, axis=-1, eps=1e-05):
    m = jnp.mean(x, axis=axis, keepdims=True)
    v = jnp.var(x, axis=axis, keepdims=True)
    return (x - m) / jnp.sqrt(v + eps)

def _scatter_add(tgt, idx, src, axis=0):
    return tgt.at[idx].add(src)

def _segment_sum(src, seg, n):
    return jax.ops.segment_sum(src, seg, n)
kernel_name = 'mk_macaron_d1_jaxref_r8_480ff3'

def setup_inputs(seed: int=0):
    np.random.seed(seed)
    _w = jnp.asarray

    def _L0_attn_setup():
        import jax, jax.numpy as jnp
        import numpy as np
        N_EMBD = 128
        N_HEAD = 16
        SEQ = 256
        BATCH = 2
        NEG = -1000000000.0
        key = jax.random.key(seed)
        k0, k1, k2 = jax.random.split(key, 3)
        return {'hidden_states': jax.random.normal(k0, (BATCH, SEQ, N_EMBD), dtype=jnp.float32), 'w_attn': jax.random.normal(k1, (3 * N_EMBD, N_EMBD), dtype=jnp.float32) * 0.02, 'b_attn': jnp.zeros((3 * N_EMBD,), dtype=jnp.float32), 'w_proj': jax.random.normal(k2, (N_EMBD, N_EMBD), dtype=jnp.float32) * 0.02, 'b_proj': jnp.zeros((N_EMBD,), dtype=jnp.float32)}
    _L0_attn_in = _L0_attn_setup()

    def _L0_ffn_setup():
        import jax, jax.numpy as jnp
        import numpy as np
        NUM_EXPERTS = 8
        IN_FEATURES = 128
        HIDDEN_FEATURES = 512
        GATE_DIM = 16
        EPS = 0.0001
        key = jax.random.key(seed)
        ks = jax.random.split(key, 7)
        hidden_states = jax.random.normal(ks[0], (1, 256, IN_FEATURES), dtype=jnp.float32)
        wg_red = jax.random.normal(ks[1], (GATE_DIM, IN_FEATURES), dtype=jnp.float32) * 0.02
        wg = jax.random.normal(ks[2], (NUM_EXPERTS, GATE_DIM), dtype=jnp.float32)
        w1 = jax.random.uniform(ks[3], (NUM_EXPERTS, IN_FEATURES, HIDDEN_FEATURES), dtype=jnp.float32)
        b1 = jax.random.uniform(ks[4], (NUM_EXPERTS, HIDDEN_FEATURES), dtype=jnp.float32)
        w2 = jax.random.uniform(ks[5], (NUM_EXPERTS, HIDDEN_FEATURES, IN_FEATURES), dtype=jnp.float32)
        b2 = jax.random.uniform(ks[6], (NUM_EXPERTS, IN_FEATURES), dtype=jnp.float32)
        return {'hidden_states': hidden_states, 'wg_red': wg_red, 'wg': wg, 'w1': w1, 'b1': b1, 'w2': w2, 'b2': b2}
    _L0_ffn_in = _L0_ffn_setup()
    _d = {'L0_attn_hidden_states': _L0_attn_in['hidden_states'], 'L0_attn_w_attn': _L0_attn_in['w_attn'], 'L0_attn_b_attn': _L0_attn_in['b_attn'], 'L0_attn_w_proj': _L0_attn_in['w_proj'], 'L0_attn_b_proj': _L0_attn_in['b_proj'], 'L0_ffn_wg_red': _L0_ffn_in['wg_red'], 'L0_ffn_wg': _L0_ffn_in['wg'], 'L0_ffn_w1': _L0_ffn_in['w1'], 'L0_ffn_b1': _L0_ffn_in['b1'], 'L0_ffn_w2': _L0_ffn_in['w2'], 'L0_ffn_b2': _L0_ffn_in['b2']}
    _x0 = _d['L0_attn_hidden_states']
    _d['L0_attn_hidden_states'] = jax.random.normal(jax.random.fold_in(jax.random.key(seed), 1), (2, 1024, 128), dtype=_x0.dtype)
    del _x0
    return _d

def reference(L0_attn_hidden_states, L0_attn_w_attn, L0_attn_b_attn, L0_attn_w_proj, L0_attn_b_proj, L0_ffn_wg_red, L0_ffn_wg, L0_ffn_w1, L0_ffn_b1, L0_ffn_w2, L0_ffn_b2):

    def _L0_attn_ref(hidden_states, w_attn, b_attn, w_proj, b_proj):
        import jax, jax.numpy as jnp
        import numpy as np
        N_EMBD = 128
        N_HEAD = 16
        SEQ = 256
        BATCH = 2
        NEG = -1000000000.0
        B, S, E = hidden_states.shape
        H = N_HEAD
        D = E // H
        qkv = hidden_states @ w_attn.T + b_attn
        q, k, v = jnp.split(qkv, 3, axis=-1)
        split = lambda t: t.reshape(B, S, H, D).transpose(0, 2, 1, 3)
        q, k, v = (split(q), split(k), split(v))
        w = jnp.einsum('bhnd,bhmd->bhnm', q, k) * jax.lax.rsqrt(float(D))
        mask = jnp.tril(jnp.ones((S, S), dtype=jnp.float32))
        w = jnp.where(mask > 0, w, NEG)
        w = jax.nn.softmax(w, axis=-1)
        attn = jnp.einsum('bhnm,bhmd->bhnd', w, v)
        attn = attn.transpose(0, 2, 1, 3).reshape(B, S, E)
        return attn @ w_proj.T + b_proj

    def _L0_ffn_ref(hidden_states, wg_red, wg, w1, b1, w2, b2):
        import jax, jax.numpy as jnp
        import numpy as np
        NUM_EXPERTS = 8
        IN_FEATURES = 128
        HIDDEN_FEATURES = 512
        GATE_DIM = 16
        EPS = 0.0001
        b, t, c = hidden_states.shape
        x = hidden_states.reshape(-1, c)
        xr = x @ wg_red.T
        wg_unit = wg / jnp.maximum(jnp.linalg.norm(wg, axis=1, keepdims=True), EPS)
        logits = xr @ wg_unit.T
        gates = jax.nn.softmax(logits, axis=1)
        indices_s = jnp.argmax(gates, axis=1)
        scores = jnp.max(gates, axis=1)
        E = wg.shape[0]
        out = jnp.zeros_like(x)
        for e in range(E):
            mask = (indices_s == e).astype(x.dtype)[:, None]
            h = jax.nn.gelu(x @ w1[e] + b1[e], approximate=False)
            out = out + mask * (h @ w2[e] + b2[e])
        out = out * scores[:, None]
        return out.reshape(b, t, c)
    x = L0_attn_hidden_states
    x = x + 0.5 * _L0_ffn_ref(_layernorm(x, axis=-1), L0_ffn_wg_red, L0_ffn_wg, L0_ffn_w1, L0_ffn_b1, L0_ffn_w2, L0_ffn_b2)
    x = x + _L0_attn_ref(_layernorm(x, axis=-1), L0_attn_w_attn, L0_attn_b_attn, L0_attn_w_proj, L0_attn_b_proj)
    x = x + 0.5 * _L0_ffn_ref(_layernorm(x, axis=-1), L0_ffn_wg_red, L0_ffn_wg, L0_ffn_w1, L0_ffn_b1, L0_ffn_w2, L0_ffn_b2)
    return x

_drawn_inputs = setup_inputs


def setup_inputs(seed=0):
    import zlib

    import numpy as np

    out = dict(_drawn_inputs(seed))
    spreads = {'L0_attn_b_attn': (0.0, 0.8), 'L0_attn_b_proj': (0.0, 1.42)}
    factors = {'L0_attn_w_attn': 8.0, 'L0_attn_w_proj': 8.0, 'L0_ffn_b1': 4.076, 'L0_ffn_b2': 27.189}
    for name, (base, spread) in spreads.items():
        noise = np.random.default_rng([zlib.crc32(name.encode()), seed]).standard_normal(out[name].shape)
        drawn = base * np.exp(spread * noise) if base else spread * noise
        out[name] = jnp.asarray(drawn.astype(out[name].dtype))
    for name, factor in factors.items():
        out[name] = (out[name] * factor).astype(out[name].dtype)
    return out
```

```python
from contextlib import ExitStack

import concourse.bass as bass
from concourse import mybir

F32 = mybir.dt.float32
BF16 = mybir.dt.bfloat16
I32 = mybir.dt.int32
ALU = mybir.AluOpType
ACT = mybir.ActivationFunctionType
AX_X = mybir.AxisListType.X

P = 128


def macaron_kernel(nc, x, w_attn, b_attn, w_proj, b_proj, wg_red, wg, w1, b1, w2, b2, out):
    BATCH, SEQ, D = x.shape
    TOK = BATCH * SEQ
    NT = TOK // P
    E, G = wg.shape
    HID = w1.shape[2]
    HC = HID // P
    ST = NT + E - 1
    ROW = D + 4
    LN_EPS, NORM_EPS = 1e-5, 1e-4
    H, HD = 16, D // 16
    HG = 4
    NG = BATCH * H // HG
    KB = SEQ // P
    PARTS = 3
    TERMS = PARTS * PARTS * HD
    SCALE = float(HD) ** -0.5
    MASKED = -1.0e30
    assert KB == 8 and NG == 8 and HD == 8
    assert D == P and HC * P == HID and ST % 2 == 1

    x_rows = x.rearrange("b (t p) d -> b p t d", p=P)
    out_rows = out.rearrange("b (t p) d -> b p t d", p=P)
    routed = [nc.dram_tensor(f"routed{k}", (ST * P, ROW), F32, kind="Internal").ap() for k in range(2)]
    expert_out = [nc.dram_tensor(f"expert_out{k}", (TOK + ST * P, D), F32, kind="Internal").ap() for k in range(2)]

    q_parts = nc.dram_tensor("q_parts", (NG * HG, PARTS * HD, SEQ), BF16, kind="Internal").ap()
    k_parts = nc.dram_tensor("k_parts", (NG * HG, (2 * PARTS - 1) * HD, SEQ), BF16, kind="Internal").ap()

    ROW_CHUNKS = [[(7, 0, 512, 0)], [(7, 512, 512, 0)], [(6, 0, 512, 0)], [(6, 512, 384, 0), (0, 0, 128, 384)],
                  [(5, 0, 512, 0)], [(5, 512, 256, 0), (1, 0, 256, 256)], [(4, 0, 512, 0)],
                  [(4, 512, 128, 0), (2, 0, 384, 128)], [(3, 0, 512, 0)]]
    ROW_MAXIMA = {7: (0, 8), 6: (8, 15), 0: (15, 16), 5: (16, 22), 1: (22, 24), 4: (24, 29), 2: (29, 32), 3: (32, 36)}
    RC = len(ROW_CHUNKS)

    def key_chunk(t):
        if t >= 16:
            return [(2 * (t - 16) + e, 4, 512 * e - 512) for e in range(2)]
        j = t // 4
        return [(t % 4, j, -128 * j)] + ([(t % 4, 8 - j, 0)] if j else [])
    CH = 18
    PIECES = [(0, 0, 256), (0, 256, 256), (0, 512, 256), (0, 768, 256),
              (1, 128, 384), (1, 512, 256), (1, 768, 256), (7, 896, 128),
              (2, 256, 256), (2, 512, 256), (2, 768, 256), (6, 768, 256),
              (3, 384, 128), (3, 512, 256), (3, 768, 256), (5, 640, 384),
              (4, 512, 256), (4, 768, 256)]
    LAG = 5
    HALF_DONE = (13, 18)
    PROBS = 9

    def last_piece(t):
        return CH - 1 if t >= 16 else 4 * (t // 4) + 3

    ROW_TURNS = [("rows", k // RC, k % RC) for k in range(HG * RC)]
    OUT_STEP, MAXIMA_STEP = (1, 6), (9, 17)

    def turns_at(t, first=False, last=False):
        out = [("out", h) for h in range(2) if OUT_STEP[h] == t and not first]
        if not last:
            out += [r for k, r in enumerate(ROW_TURNS) if k * 16 // len(ROW_TURNS) == t]
            out += [("maxima", h) for h in range(2) if MAXIMA_STEP[h] == t]
        return out
    PRO_TURNS = ROW_TURNS[:18] + ROW_TURNS[18:20] + [("maxima", 0)] + ROW_TURNS[20:] + [("maxima", 1)]
    GT = len(ROW_TURNS) + 4

    def turns_before(g):
        return g * GT + (2 * len(PRO_TURNS) - GT)

    class Group:
        def __init__(self, n, slot, turn):
            self.n, self.slot, self.turn = n, slot, turn

        def plus(self, d):
            return Group(self.n + d, (self.slot + d) % 3, self.turn + (self.slot + d) // 3)

    with ExitStack() as ctx:
        def sb(name, shape, dt=F32):
            return ctx.enter_context(nc.sbuf_tensor(name, shape, dt))

        def sem(name):
            return ctx.enter_context(nc.semaphore(name))

        ident = sb("ident", [P, P])
        ones_bf = sb("ones_bf", [P, P], BF16)
        before_bf = sb("before_bf", [P, P], BF16)
        rank_weight = sb("rank_weight", [P, E])
        tile_starts = sb("tile_starts", [P, E, NT])
        slot_tile_no = sb("slot_tile_no", [P, ST, E])
        blank_all = sb("blank_all", [P, max(ST * ROW, PARTS * SEQ)])
        blank = blank_all[:, 0:ST * ROW].rearrange("p (s r) -> p s r", r=ROW)

        W1 = sb("W1", [P, E * HID])
        W2 = sb("W2", [P, E * HC * D])
        b1_rows = sb("b1_rows", [E * HC, P])
        b1_cols = sb("b1_cols", [P, E * HC])
        b2_all = sb("b2_all", [P, E * D])
        wg_red_sb = sb("wg_red_sb", [G, D])
        wg_sb = sb("wg_sb", [E, G])
        wg_sq = sb("wg_sq", [E, G])
        wg_norm = sb("wg_norm", [E, 8])
        wg_unit = sb("wg_unit", [E, G])
        wg_unit_t = sb("wg_unit_t", [G, E])
        gate_w = sb("gate_w", [P, E])

        X = sb("X", [P, NT, D])
        XR = sb("XR", [P, NT, ROW])
        XT = sb("XT", [P, TOK])
        YT = sb("YT", [P, NT, D])
        w_attn_sb = sb("w_attn_sb", [P, 3, D])
        w_proj_sb = sb("w_proj_sb", [P, D])
        w_attn_t = sb("w_attn_t", [P, 3 * D])
        w_proj_t = sb("w_proj_t", [P, D])
        b_attn_rows = sb("b_attn_rows", [3, D])
        b_attn_cols = sb("b_attn_cols", [P, 3])
        b_v = sb("b_v", [P, D])
        b_p = sb("b_p", [P, D])
        ident_bf = sb("ident_bf", [P, P], BF16)
        row_mask = sb("row_mask", [P, P], BF16)
        key_mask = sb("key_mask", [P, P], BF16)
        QK = sb("QK", [P, 3, 2, HG, SEQ], BF16)
        probs = sb("probs", [P, PROBS, SEQ])
        V = sb("V", [P, NG, KB, HG * HD])
        VS = sb("VS", [P, 3, KB, HG, 32])
        block_max = sb("block_max", [P, HG, 4 * RC])
        neg_max = [sb(f"neg_max{i}", [P, 2, KB]) for i in range(2)]
        neg_rest = [sb(f"neg_rest{i}", [P, 2, KB]) for i in range(2)]
        neg_parts_all = [sb(f"neg_parts{i}", [P, P], BF16) for i in range(2)]
        neg_parts = [a[:, 0:PARTS * 2 * KB].rearrange("p (a h i) -> p a h i", a=PARTS, h=2) for a in neg_parts_all]
        neg_rows = [sb(f"neg_rows{i}", [PARTS * 2 * KB, P], BF16) for i in range(2)]
        inv_sum = [sb(f"inv_sum{i}", [P, 4, HG]) for i in range(2)]
        stats = sb("stats", [P, NT, 6])
        mean_var = sb("mean_var", [P, NT, 2])
        var_eps = sb("var_eps", [P, NT])
        std = sb("std", [P, NT])
        rstd = sb("rstd", [P, NT])
        nt_a = sb("nt_a", [P, NT])
        nt_b = sb("nt_b", [P, NT])

        gt = [sb(f"gt{i}", [P, NT, E]) for i in range(4)]
        gmax = sb("gmax", [P, NT])
        gsum = sb("gsum", [P, NT])
        half_score = sb("half_score", [P, NT])
        onehot = sb("onehot", [P, NT, E], BF16)
        cum = [sb(f"cum{i}", [P, NT + NT // 2, E]) for i in range(2)]
        etiles = sb("etiles", [P, E])
        etiles_end = sb("etiles_end", [P, E])
        ebase = sb("ebase", [P, E])
        starts_gt = sb("starts_gt", [P, E, NT])
        slot_f = sb("slot_f", [P, NT])
        slot = sb("slot", [P, NT], I32)
        tile_ge = sb("tile_ge", [P, ST, E])
        tile_expert_f = sb("tile_expert_f", [P, ST])
        tile_expert = sb("tile_expert", [P, ST + 3], I32)

        shared = QK[:, :, :, :, :].rearrange("p a b c d -> p (a b c d)").bitcast(F32)
        taken = [0]

        def of_shared(width):
            taken[0] += width
            return shared[:, taken[0] - width:taken[0]]
        XS = [of_shared(ROW) for i in range(4)]
        XST = [of_shared(P) for i in range(2)]
        W1S = [of_shared(HID) for i in range(2)]
        HB = [of_shared(HID) for i in range(2)]
        HT = [of_shared(HID) for i in range(2)]
        YB = [of_shared(D) for i in range(2)]
        token_nos = sb("token_nos", [P, ST], I32)
        token_no = [sb(f"token_no{i}", [P, 1], I32) for i in range(2)]

        qk_f = [YT[:, 8 * i:8 * i + 4, :].rearrange("p a d -> p (a d)") for i in range(2)]
        qk_r = [YT[:, 8 * i + 4:8 * i + 8, :].rearrange("p a d -> p (a d)") for i in range(2)]
        blank_bf = blank_all[:, :].bitcast(BF16)
        qk_split = [blank_bf[:, 3072 * z:3072 * (z + 1)].rearrange("p (a t) -> p a t", a=PARTS) for z in range(2)]
        attn = YT[:, :, :].rearrange("p t d -> p (t d)")
        out_t = XT[:, 0:SEQ]
        attn_t = XT[:, :]

        PS = ctx.enter_context(nc.psum_tensor("PS", [P, 8 * 512], F32))
        PB = [PS[:, 512 * i:512 * (i + 1)] for i in range(8)]
        turn_bank = [PB[0], PB[1]]
        key_scores = [PS[:, 1024:2048], PS[:, 2048:3072]]
        out_acc = PS[:, 3072:4096]

        x_loaded = [sem(f"x_loaded{b}") for b in range(BATCH)]
        small_loaded = sem("small_loaded")
        w1_loaded, w2_loaded = sem("w1_loaded"), sem("w2_loaded")
        consts_made = sem("consts_made")
        pool_step = sem("pool_step")
        dve_step = sem("dve_step")
        blanked = [sem(f"blanked{k}") for k in range(2)]
        wgu_t_done, gate_w_done, b1_t_done = sem("wgu_t_done"), sem("gate_w_done"), sem("b1_t_done")
        norm_var, norm_std = sem("norm_var"), sem("norm_std")
        norm_rows = sem("norm_rows")
        rows_turned, turned_kept = sem("rows_turned"), sem("turned_kept")
        logits_done, logits_less_max, gates_exp = sem("logits_done"), sem("logits_less_max"), sem("gates_exp")
        onehot_ready, counts_done = sem("onehot_ready"), sem("counts_done")
        slots_ready, experts_ready = sem("slots_ready"), sem("experts_ready")
        rows_routed = sem("rows_routed")
        xs_loaded = [sem(f"xs_loaded{i}") for i in range(4)]
        xs_turned, xst_kept = sem("xs_turned"), sem("xst_kept")
        w1_staged = sem("w1_staged")
        up_done, up_biased, gelu_done = sem("up_done"), sem("up_biased"), sem("gelu_done")
        down_done, y_ready = sem("down_done"), sem("y_ready")
        token_no_kept, token_no_at_pool = sem("token_no_kept"), sem("token_no_at_pool")
        y_sent = [sem(f"y_sent{i}") for i in range(2)]
        y_back = sem("y_back")
        attn_w_done, attn_w_kept = sem("attn_w_done"), sem("attn_w_kept")
        qk_done, qk_kept, part0_ready, rest_ready, part1_ready = (sem(n) for n in ("qk_done", "qk_kept", "part0_ready", "rest_ready", "part1_ready"))
        parts_ready, parts_sent = sem("parts_ready"), [sem(f"parts_sent{z}") for z in range(2)]
        v_done, v_kept, v_staged = sem("v_done"), sem("v_kept"), sem("v_staged")
        qk_loaded = [sem(f"qk_loaded{i}") for i in range(3)]
        ones_set = sem("ones_set")
        turn_done, turn_used = sem("turn_done"), sem("turn_used")
        max_step, max_parts_ready = sem("max_step"), sem("max_parts_ready")
        max_sent = [sem(f"max_sent{h}") for h in range(2)]
        scores_done, probs_ready, pieces_done, out_kept, sums_inverted = (sem(n) for n in ("scores_done", "probs_ready", "pieces_done", "out_kept", "sums_inverted"))
        attn_turned, attn_kept, proj_done = sem("attn_turned"), sem("attn_kept"), sem("proj_done")
        bias_added, attended = sem("bias_added"), sem("attended")
        result_ready, stored = sem("result_ready"), sem("stored")

        def loaded(k, q, m):
            return q * 16 + 16 * (k * ((ST - 1 - m) // 4 + 1) + 1)

        def sent(k, q, m, more=0):
            return q * 32 + 16 * (k * ((ST + 1 - m % 2) // 2) + m // 2 + more)

        def after(q, m, d):
            return q + (m + d) // 4, (m + d) % 4

        def experts_of(engine, registers):
            def load(q):
                engine.load(registers, tile_expert[0:1, bass.ds(q * 4, 6)])
                return [engine.snap(r, min_val=0, max_val=E - 1) for r in registers]
            return load

        def tile_pipeline(engine, steps, begin=lambda q: None):
            at_q = begin(0)
            for m in range(4):
                steps(0, m, m, None, at_q)
            with engine.Fori(1, (ST - 3) // 4) as q:
                at_q = begin(q)
                for m in range(4):
                    steps(q, m, None, None, at_q)
            at_q = begin((ST - 3) // 4)
            for m in range(3):
                steps((ST - 3) // 4, m, None, ST - 3 + m, at_q)

        def max_turn(g, half):
            if isinstance(g.n, int) and g.n == 0:
                return PRO_TURNS.index(("maxima", half)) + 1
            at = [u for t in range(CH) for u in turns_at(t)].index(("maxima", half))
            return turns_before(g.n - 1) + (at + 1)

        def out_turn(g, half):
            at = [u for t in range(CH) for u in turns_at(t)].index(("out", half))
            return turns_before(g.n + 1) + (at + 1)

        def group_pipeline(engine, steps):
            steps(Group(0, 0, 0), True, False)
            with engine.Fori(0, (NG - 2) // 3) as i:
                for j in range(3):
                    steps(Group(i * 3 + (1 + j), (1 + j) % 3, i + (1 + j) // 3), False, False)
            steps(Group(NG - 1, (NG - 1) % 3, (NG - 1) // 3), False, True)

        block = ctx.enter_context(nc.Block())

        @block.sync
        def _(sp):
            for b in range(BATCH):
                sp.dma_start(X[:, b * NT // BATCH:(b + 1) * NT // BATCH, :], x_rows[b]).then_inc(x_loaded[b], 16)
            sp.dma_start(wg_red_sb[:, :], wg_red).then_inc(small_loaded, 16)
            sp.dma_start(wg_sb[:, :], wg).then_inc(small_loaded, 16)
            sp.dma_start(b1_rows[:, :], b1.rearrange("e (c p) -> (e c) p", p=P)).then_inc(small_loaded, 16)
            sp.dma_start(b2_all[:, :], b2.rearrange("(o e) d -> o (e d)", o=1).broadcast_to([P, E * D])).then_inc(small_loaded, 16)
            sp.dma_start(w_attn_sb[:, :, :], w_attn.rearrange("(a p) d -> p a d", p=P)).then_inc(small_loaded, 16)
            sp.dma_start(w_proj_sb[:, :], w_proj).then_inc(small_loaded, 16)
            sp.dma_start(b_attn_rows[:, :], b_attn.rearrange("(a d) -> a d", a=3)).then_inc(small_loaded, 16)
            sp.dma_start(b_v[:, :], b_attn[2 * D:3 * D].rearrange("(o d) -> o d", o=1).broadcast_to([P, D])).then_inc(small_loaded, 16)
            sp.dma_start(b_p[:, :], b_proj.rearrange("(o d) -> o d", o=1).broadcast_to([P, D])).then_inc(small_loaded, 16)
            sp.wait_ge(consts_made, 1)
            for k in range(2):
                sp.dma_start(routed[k].rearrange("(s p) r -> p s r", p=P), blank[:, :, :]).then_inc(blanked[k], 16)
            sp.dma_start(W1[:, :].rearrange("p (e h) -> p e h", e=E), w1.rearrange("e p h -> p e h")).then_inc(w1_loaded, 16)
            sp.dma_start(W2[:, :].rearrange("p (e c d) -> p e c d", e=E, c=HC), w2.rearrange("e (c p) d -> p e c d", p=P)).then_inc(w2_loaded, 16)

            def ffn(k):
                B = k * ST

                def load(q, m, first, last, _):
                    s = q * 4 + m
                    if first is None:
                        sp.wait_ge(xs_turned, s + (B - 3))
                        sp.wait_ge(token_no_kept, s + (B - 3))
                    sp.dma_start(XS[m][:, :], routed[k][bass.ds(s * P, P), :]).then_inc(xs_loaded[m], 16)
                sp.wait_ge(rows_routed, 16 * NT * (k + 1))
                tile_pipeline(sp, load)
                for par in range(2):
                    sp.wait_ge(y_sent[par], 16 * (k + 1) * ((ST + 1 - par) // 2))
                sp.dma_start(YT[:, :, :], expert_out[k][0:TOK, :].rearrange("(t p) d -> p t d", p=P)).then_inc(y_back, 16)

            def attention():
                for b in range(BATCH):
                    for z, parts in ((0, q_parts), (1, k_parts)):
                        sp.wait_ge(parts_ready, 4 * b + 2 * z + 2)
                        for block_no in range(PARTS if z == 0 else 2 * PARTS - 1):
                            sp.dma_start(parts[b * H:(b + 1) * H, block_no * HD:(block_no + 1) * HD, :],
                                         qk_split[z][:, block_no % PARTS, :]).then_inc(parts_sent[z], 16)

                def load(g):
                    for r in range(PARTS):
                        sp.dma_start(QK[24 * r:24 * r + 24, g.slot, 0, :, :],
                                     q_parts[bass.ds(g.n * HG, HG), :, :].rearrange("h r t -> r h t")).then_inc(qk_loaded[g.slot], 16)
                        sp.dma_start(QK[24 * r:24 * r + 24, g.slot, 1, :, :],
                                     k_parts[bass.ds(g.n * HG, HG), 8 * r:8 * r + 24, :].rearrange("h r t -> r h t")).then_inc(qk_loaded[g.slot], 16)

                def send_max(g, half):
                    sp.wait_ge(turn_used, max_turn(g, half))
                    sp.dma_start(QK[TERMS:TERMS + PARTS, g.slot, 0, 2 * half:2 * half + 2, :], neg_rows[half][:, :]).then_inc(max_sent[half], 16)
                sp.wait_ge(parts_sent[0], 16 * PARTS * BATCH)
                sp.wait_ge(parts_sent[1], 16 * (2 * PARTS - 1) * BATCH)
                sp.wait_ge(ones_set, 1)
                load(Group(0, 0, 0))
                load(Group(1, 1, 0))
                for half in range(2):
                    send_max(Group(0, 0, 0), half)
                with sp.Fori(0, (NG - 2) // 3) as i:
                    for j in range(3):
                        g = Group(i * 3 + j, j, i)
                        sp.wait_ge(scores_done, g.n * CH + 1)
                        load(g.plus(2))
                        for half in range(2):
                            send_max(g.plus(1), half)
                for half in range(2):
                    send_max(Group(NG - 1, (NG - 1) % 3, (NG - 1) // 3), half)
            ffn(0)
            attention()
            ffn(1)
            sp.wait_ge(result_ready, 2)
            for b in range(BATCH):
                sp.dma_start(out_rows[b], X[:, b * NT // BATCH:(b + 1) * NT // BATCH, :]).then_inc(stored, 16)
            sp.wait_ge(stored, 16 * BATCH)

        @block.gpsimd
        def _(pool):
            n = [0]

            def step(ins):
                n[0] += 1
                ins.then_inc(pool_step, 1)
                pool.wait_ge(pool_step, n[0])

            step(pool.memset(blank[:, :, :], 0.0))
            step(pool.iota(blank[:, :, D:D + 1].bitcast(I32).rearrange("p s o -> p (s o)"), [[P, ST]], base=TOK, channel_multiplier=1))
            pool.memset(ones_bf[:, :], 1.0).then_inc(consts_made, 1)
            step(pool.memset(ident[:, :], 0.0))
            step(pool.affine_select(out=ident[:, :], in_=ident[:, :], compare_op=ALU.not_equal, fill=1.0, base=0, pattern=[[-1, P]], channel_multiplier=1))
            step(pool.memset(before_bf[:, :], 1.0))
            step(pool.affine_select(out=before_bf[:, :], in_=before_bf[:, :], compare_op=ALU.is_gt, fill=0.0, base=0, pattern=[[1, P]], channel_multiplier=-1))
            step(pool.memset(row_mask[:, :], 0.0))
            step(pool.affine_select(out=row_mask[:, :], in_=row_mask[:, :], compare_op=ALU.is_ge, fill=MASKED, base=0, pattern=[[-1, P]], channel_multiplier=1))
            step(pool.memset(key_mask[:, :], 0.0))
            step(pool.affine_select(out=key_mask[:, :], in_=key_mask[:, :], compare_op=ALU.is_ge, fill=MASKED, base=0, pattern=[[1, P]], channel_multiplier=-1))
            step(pool.tensor_copy(ident_bf[:, :], ident[:, :]))
            step(pool.memset(VS[:, :, :, :, :], 0.0))
            for half in range(2):
                step(pool.memset(neg_parts_all[half][:, :], 0.0))
            step(pool.memset(VS[:, :, :, :, HD:HD + 1], 1.0))
            step(pool.iota(rank_weight[:, :], [[-1, E]], base=E, channel_multiplier=0, allow_small_or_imprecise_dtypes=True))
            step(pool.iota(tile_starts[:, :, :], [[0, E], [P, NT]], base=0, channel_multiplier=0, allow_small_or_imprecise_dtypes=True))
            step(pool.iota(slot_tile_no[:, :, :], [[1, ST], [0, E]], base=0, channel_multiplier=0, allow_small_or_imprecise_dtypes=True))
            step(pool.memset(cum[0][:, 0:NT // 2, :], 0.0))
            step(pool.memset(cum[1][:, 0:NT // 2, :], 0.0))
            step(pool.memset(XR[:, :, D:ROW], 0.0))
            pool.iota(XR[:, :, D:D + 1].bitcast(I32).rearrange("p s o -> p (s o)"), [[P, NT]], base=0, channel_multiplier=1).then_inc(consts_made, 1)

            def ffn(k):
                B = k * ST
                pool.wait_ge(slots_ready, k + 1)
                pool.wait_ge(blanked[k], 16)
                for t in range(NT):
                    pool.indirect_dma_start(routed[k], bass.IndirectOffsetOnAxis(ap=slot[:, t:t + 1], axis=0),
                                            XR[:, t, :], None).then_inc(rows_routed, 16)

                def send(q, m, first, last, _):
                    s, par = q * 4 + m, m % 2
                    pool.wait_ge(token_no_kept, s + (B + 1))
                    if first is None or first >= 2:
                        pool.wait_ge(y_sent[par], sent(k, q, m))
                    pool.tensor_copy(token_no[par][:, :], token_nos[:, bass.ds(s, 1)]).then_inc(token_no_at_pool, 1)
                    pool.wait_ge(slots_ready, k + 1)
                    pool.wait_ge(token_no_at_pool, s + (B + 1))
                    pool.wait_ge(y_ready, s + (B + 1))
                    pool.indirect_dma_start(expert_out[k], bass.IndirectOffsetOnAxis(ap=token_no[par][:, 0:1], axis=0),
                                            YB[par][:, :], None).then_inc(y_sent[par], 16)
                tile_pipeline(pool, send)

            def attention():
                for item in range(4 * BATCH):
                    b, z, c = item // 4, item // 2 % 2, item % 2
                    pool.wait_ge(rest_ready, item + 1)
                    pool.tensor_copy(qk_split[z][:, 1, 512 * c:512 * (c + 1)], qk_r[item % 2]).then_inc(part1_ready, 1)
                pool.wait_ge(norm_rows, 2 * NT)
                pool.tensor_tensor(X[:, :, :], X[:, :, :], b_p[:, :].unsqueeze(1).broadcast_to([P, NT, D]), ALU.add).then_inc(bias_added, 1)

                def stage(g):
                    pool.tensor_copy(VS[:, g.slot, :, :, 0:HD], V[:, :, :, :].rearrange("p g i f -> p (g i f)")[:, bass.ds(g.n * (KB * HG * HD), KB * HG * HD)]
                                     .rearrange("p (i h d) -> p i h d", i=KB, h=HG)).then_inc(v_staged, 1)
                pool.wait_ge(v_kept, 4)
                stage(Group(0, 0, 0))
                stage(Group(1, 1, 0))
                with pool.Fori(0, (NG - 2) // 3) as i:
                    for j in range(3):
                        g = Group(i * 3 + j, j, i)
                        pool.wait_ge(pieces_done, g.n * CH + 1)
                        stage(g.plus(2))
            ffn(0)
            attention()
            ffn(1)

        @block.scalar
        def _(act):
            def norm(q):
                act.wait_ge(norm_var, q + 1)
                act.activation(std[:, :], var_eps[:, :], ACT.Sqrt).then_inc(norm_std, 1)

            def keep_rows(q):
                for c in range(4):
                    act.wait_ge(rows_turned, 4 * q + c + 1)
                    act.activation(XT[:, c * 512:(c + 1) * 512], PB[c][:, :], ACT.Copy).then_inc(turned_kept, 1)

            def ffn(k):
                B = k * ST
                keep_rows(2 * k)
                act.wait_ge(logits_less_max, k + 1)
                act.activation(gt[1][:, :, :], gt[0][:, :, :], ACT.Exp).then_inc(gates_exp, 1)

                def keep_turned(q, m, first):
                    s, par = q * 4 + m, m % 2
                    act.wait_ge(xs_turned, s + (B + 1))
                    if first is None or first >= 2:
                        act.wait_ge(up_done, s + (B - 1))
                    act.activation(XST[par][:, :], PB[par][:, 0:P], ACT.Copy).then_inc(xst_kept, 1)
                    act.activation(token_nos[:, bass.ds(s, 1)], XS[m][:, D:D + 1].bitcast(I32), ACT.Copy).then_inc(token_no_kept, 1)

                def gelu(q, m, first):
                    s, par = q * 4 + m, m % 2
                    act.wait_ge(up_biased, s + (B + 1))
                    if first is None or first >= 2:
                        act.wait_ge(down_done, s + (B - 1))
                    act.activation(HT[par][:, :], HB[par][:, :], ACT.Gelu).then_inc(gelu_done, 1)

                def steps(q, m, first, last, experts):
                    if last != ST - 1:
                        keep_turned(*after(q, m, 1), None if first is None else first + 1)
                    gelu(q, m, first)
                keep_turned(0, 0, 0)
                tile_pipeline(act, steps)
            def attention():
                keep_rows(1)
                for item in range(4 * BATCH):
                    b, z, c = item // 4, item // 2 % 2, item % 2
                    act.wait_ge(qk_done, item + 1)
                    if item >= 2:
                        act.wait_ge(rest_ready, item - 1)
                    act.activation(qk_f[item % 2], PB[4 + item % 4], ACT.Identity, bias=b_attn_cols[:, z:z + 1]).then_inc(qk_kept, 1)
                    act.wait_ge(qk_kept, item + 1)
                    if b and c == 0:
                        act.wait_ge(parts_sent[z], 16 * (PARTS if z == 0 else 2 * PARTS - 1))
                    act.activation(qk_split[z][:, 0, 512 * c:512 * (c + 1)], qk_f[item % 2], ACT.Copy).then_inc(part0_ready, 1)

                def keep_out(g, half, final=False):
                    act.wait_ge(pieces_done, g.n * CH + HALF_DONE[half])
                    act.wait_ge(turn_done, turns_before(NG - 1) + half + 1 if final else out_turn(g, half) - GT)
                    act.activation(out_t[:, 512 * half:512 * (half + 1)], out_acc[:, 512 * half:512 * (half + 1)], ACT.Copy).then_inc(out_kept, 1)

                def steps(g, first, last):
                    for t in range(CH):
                        if not first and t == 0:
                            keep_out(g.plus(-1), 0)
                        if not first and t == LAG:
                            keep_out(g.plus(-1), 1)
                        act.wait_ge(scores_done, g.n * CH + (t + 1))
                        if t >= PROBS:
                            act.wait_ge(pieces_done, g.n * CH + (last_piece(t - PROBS) + 1))
                        elif not first:
                            act.wait_ge(pieces_done, (g.n - 1) * CH + (last_piece(t + PROBS) + 1))
                        act.activation(probs[:, t % PROBS, :], key_scores[t % 2], ACT.Exp, scale=SCALE).then_inc(probs_ready, 1)
                group_pipeline(act, steps)
                for half in range(2):
                    keep_out(Group(NG - 1, 0, 0), half, True)
                for c in range(4):
                    act.wait_ge(attn_turned, c + 1)
                    act.activation(attn_t[:, 512 * c:512 * (c + 1)], PB[2 + c], ACT.Copy).then_inc(attn_kept, 1)
            act.wait_ge(norm_var, 1)
            act.activation(wg_norm[:, 1:2], wg_norm[:, 0:1], ACT.Sqrt).then_inc(norm_std, 1)
            norm(1)
            ffn(0)
            norm(2)
            attention()
            norm(3)
            ffn(1)

        @block.tensor
        def _(pe):
            pe_experts = [pe.alloc_register(f"pe_expert{j}") for j in range(6)]
            pe.wait_ge(consts_made, 2)
            pe.wait_ge(small_loaded, 144)
            for a in range(3):
                pe.transpose(PB[4][:, a * P:(a + 1) * P], w_attn_sb[:, a, :], ident[:, :])
            pe.transpose(PB[4][:, 3 * P:4 * P], w_proj_sb[:, :], ident[:, :]).then_inc(attn_w_done, 1)
            pe.transpose(PB[5][:, 64:67], b_attn_rows[:, :], ident[0:3, 0:3])
            pe.transpose(PB[5][:, 0:E * HC], b1_rows[:, :], ident[0:E * HC, 0:E * HC]).then_inc(b1_t_done, 1)
            pe.wait_ge(wgu_t_done, 1)
            pe.transpose(PB[6][0:G, 0:E], wg_unit[:, :], ident[0:E, 0:E]).then_inc(gate_w_done, 1)
            pe.wait_ge(wgu_t_done, 2)
            pe.matmul(PB[7][:, 0:E], wg_red_sb[:, :], wg_unit_t[:, :], start=True, stop=True).then_inc(gate_w_done, 1)

            def turn_rows(q):
                for t in range(NT):
                    pe.wait_ge(norm_rows, NT * q + t + 1)
                    mm = pe.transpose(PB[t // 4][:, (t % 4) * P:(t % 4 + 1) * P], XR[:, t, 0:D], ident[:, :])
                    if t % 4 == 3:
                        mm.then_inc(rows_turned, 1)

            def ffn(k):
                B = k * ST
                turn_rows(2 * k)
                pe.wait_ge(wgu_t_done, 3)
                for t in range(NT):
                    if t % 4 == 0:
                        pe.wait_ge(turned_kept, 8 * k + t // 4 + 1)
                    mm = pe.matmul(PB[6][:, t * E:(t + 1) * E], XT[:, t * P:(t + 1) * P], gate_w[:, :], start=True, stop=True)
                mm.then_inc(logits_done, 1)
                pe.wait_ge(onehot_ready, k + 1)
                pe.matmul(PB[7][:, 0:NT * E], before_bf[:, :], onehot[:, :, :].rearrange("p t e -> p (t e)"), start=True, stop=True)
                pe.matmul(PB[7][:, 128:128 + NT * E], ones_bf[:, :], onehot[:, :, :].rearrange("p t e -> p (t e)"), start=True, stop=True).then_inc(counts_done, 1)
                pe.wait_ge(experts_ready, k + 1)
                if k == 0:
                    pe.wait_ge(w2_loaded, 16)

                def turn(q, m, first):
                    s, par = q * 4 + m, m % 2
                    pe.wait_ge(xs_loaded[m], loaded(k, q, m))
                    if first is None or first >= 2:
                        pe.wait_ge(xst_kept, s + (B - 1))
                    pe.transpose(PB[par][:, 0:P], XS[m][:, 0:D], ident[:, :]).then_inc(xs_turned, 1)

                def up(q, m, first):
                    s, par = q * 4 + m, m % 2
                    pe.wait_ge(xst_kept, s + (B + 1))
                    pe.wait_ge(w1_staged, s + (B + 1))
                    if first is None or first >= 2:
                        pe.wait_ge(up_biased, s + (B - 1))
                    for c in range(HC):
                        mm = pe.matmul(PB[2 + par][:, c * P:(c + 1) * P], W1S[par][:, c * P:(c + 1) * P], XST[par][:, :], start=True, stop=True)
                    mm.then_inc(up_done, 1)

                def down(q, m, first, e):
                    s, par = q * 4 + m, m % 2
                    pe.wait_ge(gelu_done, s + (B + 1))
                    if first is None or first >= 2:
                        pe.wait_ge(y_ready, s + (B - 1))
                    for c in range(HC):
                        mm = pe.matmul(PB[4 + par][:, 0:D], HT[par][:, c * P:(c + 1) * P], W2[:, bass.ds(e * HID + c * D, D)], start=(c == 0), stop=(c == HC - 1))
                    mm.then_inc(down_done, 1)

                def steps(q, m, first, last, experts):
                    if last != ST - 1:
                        turn(*after(q, m, 1), None if first is None else first + 1)
                    up(q, m, first)
                    if first != 0:
                        down(*after(q, m, -1), None if first is None else first - 1, experts[m])
                    if last == ST - 1:
                        down(q, m, None, experts[m + 1])
                turn(0, 0, 0)
                tile_pipeline(pe, steps, experts_of(pe, pe_experts))

            def attention():
                turn_rows(1)
                pe.wait_ge(attn_w_kept, 2)
                for item in range(4 * BATCH):
                    b, z, c = item // 4, item // 2 % 2, item % 2
                    pe.wait_ge(turned_kept, 4 + 2 * b + c + 1)
                    if item >= 4:
                        pe.wait_ge(qk_kept, item - 3)
                    pe.matmul(PB[4 + item % 4], w_attn_t[:, z * D:(z + 1) * D], XT[:, SEQ * b + 512 * c:SEQ * b + 512 * (c + 1)], start=True, stop=True).then_inc(qk_done, 1)
                for t in range(NT):
                    mm = pe.matmul(PB[t // 4][:, (t % 4) * P:(t % 4 + 1) * P], XT[:, t * P:(t + 1) * P], w_attn_t[:, 2 * D:3 * D], start=True, stop=True)
                    if t % 4 == 3:
                        mm.then_inc(v_done, 1)

                def take_turn(u, g, what):
                    bank = turn_bank[parity[0]]
                    parity[0] = 1 - parity[0]
                    if not isinstance(u, int) or u >= 2:
                        pe.wait_ge(turn_used, u - 1)
                    if what[0] == "out":
                        half = what[1]
                        pe.wait_ge(out_kept, (g.n - 1) * 2 + (half + 1))
                        for i in range(4):
                            mm = pe.transpose(bank[:, i * P:(i + 1) * P], out_t[:, 512 * half + i * P:512 * half + (i + 1) * P], ident[:, :])
                    elif what[0] == "rows":
                        h, chunk = what[1:]
                        g = g.plus(1)
                        if h == 0 and chunk == 0:
                            pe.wait_ge(qk_loaded[g.slot], g.turn * (96) + 96)
                        for n, (i, key, keys, col) in enumerate(ROW_CHUNKS[chunk]):
                            diag = key + keys == (i + 1) * P
                            last = n == len(ROW_CHUNKS[chunk]) - 1
                            mm = pe.matmul(bank[:, col:col + keys], QK[0:TERMS, g.slot, 0, h, i * P:(i + 1) * P], QK[0:TERMS, g.slot, 1, h, key:key + keys],
                                           start=(n == 0), stop=(last and not diag), skip_group_check=True)
                            if diag:
                                mm = pe.matmul(bank[:, col + keys - P:col + keys], ident_bf[:, :], row_mask[:, :], start=False, stop=last, skip_group_check=True)
                    else:
                        half = what[1]
                        pe.wait_ge(max_parts_ready, (g.n + 1) * 2 + (half + 1))
                        mm = pe.transpose(bank.bitcast(BF16)[:, 0:P], neg_parts_all[half][:, :], ident_bf[:, :])
                    mm.then_inc(turn_done, 1)

                def scores(g, t, first):
                    if t < HG and t % 2 == 0:
                        pe.wait_ge(max_sent[t // 2], g.n * 16 + 16)
                    if t >= 2 or not first:
                        pe.wait_ge(probs_ready, g.n * CH + (t - 1))
                    started = set()
                    for h, j, q0 in key_chunk(t):
                        at, query = q0 + P * j, P * j
                        while query < SEQ:
                            width = min(512 - at % 512, SEQ - query)
                            mm = pe.matmul(key_scores[t % 2][:, at:at + width], QK[0:TERMS + PARTS, g.slot, 1, h, j * P:(j + 1) * P],
                                           QK[0:TERMS + PARTS, g.slot, 0, h, query:query + width], start=(at // 512 not in started), stop=False, skip_group_check=True)
                            started.add(at // 512)
                            if query == P * j:
                                mm = pe.matmul(key_scores[t % 2][:, at:at + P], ident_bf[:, :], key_mask[:, :], start=False, stop=True, skip_group_check=True)
                            at, query = at + width, query + width
                    mm.then_inc(scores_done, 1)

                def piece(g, n, first):
                    j, query, width = PIECES[n]
                    if n == 0:
                        pe.wait_ge(v_staged, g.n + 1)
                    if n in (0, 2) and not first:
                        pe.wait_ge(out_kept, g.n * 2 - 1 + n // 2)
                    pe.wait_ge(probs_ready, g.n * CH + (CH if n >= 16 else 4 * (n // 4) + 4))
                    for h in range(HG):
                        chunk = 16 + h // 2 if n >= 16 else 4 * (n // 4) + h
                        at = query + next(q0 for hh, jj, q0 in key_chunk(chunk) if (hh, jj) == (h, j))
                        mm = pe.matmul(out_acc[32 * h:32 * h + 32, query:query + width], VS[:, g.slot, j, h, :], probs[:, chunk % PROBS, at:at + width],
                                       start=(n in (0, 2)), stop=(n in (12, 17)), skip_group_check=True, tile_position=(0, 32 * h))
                    mm.then_inc(pieces_done, 1)

                parity = [0]
                before = Group(-1, 2, -1)
                pe.wait_ge(v_kept, 4)
                pe.wait_ge(qk_kept, 4 * BATCH)
                for u, what in enumerate(PRO_TURNS):
                    take_turn(u, before, what)

                def steps(g, first, last):
                    u = 0
                    for t in range(CH):
                        scores(g, t, first)
                        for what in turns_at(t, first, last):
                            take_turn((len(PRO_TURNS) if first else turns_before(g.n)) + u, g, what)
                            u += 1
                        if t >= LAG:
                            piece(g, t - LAG, first)
                        elif not first:
                            piece(g.plus(-1), t - LAG + CH, False)
                group_pipeline(pe, steps)
                g = Group(NG - 1, (NG - 1) % 3, (NG - 1) // 3)
                for n in range(CH - LAG, CH):
                    piece(g, n, False)
                for half in range(2):
                    take_turn(turns_before(NG - 1) + 2 + half, g.plus(1), ("out", half))
                pe.wait_ge(turn_used, turns_before(NG - 1) + 4)
                for t in range(NT):
                    mm = pe.transpose(PB[2 + t // 4][:, (t % 4) * P:(t % 4 + 1) * P], attn[:, t * D:(t + 1) * D], ident[:, :])
                    if t % 4 == 3:
                        mm.then_inc(attn_turned, 1)
                for t in range(NT):
                    if t % 4 == 0:
                        pe.wait_ge(attn_kept, t // 4 + 1)
                    bank = (6, 7, 0, 1)[t // 4]
                    mm = pe.matmul(PB[bank][:, (t % 4) * P:(t % 4 + 1) * P], attn_t[:, t * P:(t + 1) * P], w_proj_t[:, :], start=True, stop=True)
                    if t % 4 == 3:
                        mm.then_inc(proj_done, 1)
            ffn(0)
            attention()
            ffn(1)

        @block.vector
        def _(dve):
            n = [0]
            dve_experts = [dve.alloc_register(f"dve_expert{j}") for j in range(6)]

            def step(ins):
                n[0] += 1
                ins.then_inc(dve_step, 1)
                dve.wait_ge(dve_step, n[0])

            def refine_rsqrt(r, v, s, a, b):
                step(dve.reciprocal(r, s))
                step(dve.tensor_tensor(a, r, r, ALU.mult))
                step(dve.tensor_tensor(b, a, v, ALU.mult))
                step(dve.tensor_scalar(a, b, -0.5, 1.5, ALU.mult, ALU.add))
                step(dve.tensor_tensor(r, r, a, ALU.mult))

            def norm(q, var_at):
                for t in range(NT):
                    if q == 0 and t % (NT // BATCH) == 0:
                        dve.wait_ge(x_loaded[t // (NT // BATCH)], 16)
                    ins = dve.bn_stats(stats[:, t, :], X[:, t, :])
                step(ins)
                for t in range(NT):
                    ins = dve.bn_aggr(mean_var[:, t, :], stats[:, t, :])
                step(ins)
                dve.tensor_scalar(var_eps[:, :], mean_var[:, :, 1], LN_EPS, None, ALU.add).then_inc(norm_var, 1)
                dve.wait_ge(norm_std, var_at)
                dve.wait_ge(norm_var, var_at)
                refine_rsqrt(rstd[:, :], var_eps[:, :], std[:, :], nt_a[:, :], nt_b[:, :])
                dve.wait_ge(consts_made, 2)
                for t in range(NT):
                    dve.tensor_scalar(XR[:, t, 0:D], X[:, t, :], mean_var[:, t, 0:1], rstd[:, t:t + 1], ALU.subtract, ALU.mult).then_inc(norm_rows, 1)

            def by_tile(a):
                return a.unsqueeze(2).broadcast_to([P, NT, E])

            def route(k):
                dve.wait_ge(logits_done, k + 1)
                logits = PB[6][:, 0:NT * E].rearrange("p (t e) -> p t e", e=E)
                step(dve.tensor_reduce(gmax[:, :], logits, AX_X, ALU.max))
                dve.tensor_tensor(gt[0][:, :, :], logits, by_tile(gmax[:, :]), ALU.subtract).then_inc(logits_less_max, 1)
                dve.wait_ge(gates_exp, k + 1)
                step(dve.tensor_reduce(gsum[:, :], gt[1][:, :, :], AX_X, ALU.add))
                step(dve.reciprocal(gsum[:, :], gsum[:, :]))
                step(dve.tensor_tensor(gt[2][:, :, :], gt[1][:, :, :], by_tile(gsum[:, :]), ALU.mult))
                step(dve.tensor_reduce(gmax[:, :], gt[2][:, :, :], AX_X, ALU.max))
                dve.tensor_scalar(half_score[:, :], gmax[:, :], 0.5, None, ALU.mult)
                step(dve.tensor_tensor(gt[3][:, :, :], gt[2][:, :, :], by_tile(gmax[:, :]), ALU.is_ge))
                step(dve.tensor_tensor(gt[2][:, :, :], gt[3][:, :, :], rank_weight[:, :].unsqueeze(1).broadcast_to([P, NT, E]), ALU.mult))
                step(dve.tensor_reduce(gsum[:, :], gt[2][:, :, :], AX_X, ALU.max))
                dve.tensor_tensor(onehot[:, :, :], gt[2][:, :, :], by_tile(gsum[:, :]), ALU.is_equal).then_inc(onehot_ready, 1)
                Z = NT // 2
                dve.wait_ge(counts_done, k + 1)
                earlier = PB[7][:, 0:NT * E].rearrange("p (t e) -> p t e", e=E)
                counts = PB[7][:, 128:128 + NT * E].rearrange("p (t e) -> p t e", e=E)
                step(dve.tensor_copy(cum[0][:, Z:Z + NT, :], counts))
                a = 0
                shift = 1
                while shift < NT:
                    step(dve.tensor_tensor(cum[1 - a][:, Z:Z + NT, :], cum[a][:, Z:Z + NT, :], cum[a][:, Z - shift:Z - shift + NT, :], ALU.add))
                    a = 1 - a
                    shift *= 2
                step(dve.tensor_tensor(starts_gt[:, :, :], tile_starts[:, :, :], cum[a][:, Z + NT - 1, :].unsqueeze(2).broadcast_to([P, E, NT]), ALU.is_lt))
                step(dve.tensor_reduce(etiles[:, :], starts_gt[:, :, :], AX_X, ALU.add))
                step(dve.tensor_tensor_scan(etiles_end[:, :], ident_ones, etiles[:, :], 0.0, ALU.mult, ALU.add))
                step(dve.tensor_tensor(ebase[:, :], etiles_end[:, :], etiles[:, :], ALU.subtract))
                step(dve.tensor_scalar(ebase[:, :], ebase[:, :], float(P), None, ALU.mult))
                step(dve.tensor_tensor(gt[0][:, :, :], earlier, cum[a][:, Z - 1:Z - 1 + NT, :], ALU.add))
                step(dve.tensor_tensor(gt[1][:, :, :], gt[0][:, :, :], ebase[:, :].unsqueeze(1).broadcast_to([P, NT, E]), ALU.add))
                step(dve.tensor_tensor(gt[2][:, :, :], gt[1][:, :, :], onehot[:, :, :], ALU.mult))
                step(dve.tensor_reduce(slot_f[:, :], gt[2][:, :, :], AX_X, ALU.add))
                dve.tensor_copy(slot[:, :], slot_f[:, :]).then_inc(slots_ready, 1)
                step(dve.tensor_tensor(tile_ge[:, :, :], slot_tile_no[:, :, :], etiles_end[:, :].unsqueeze(1).broadcast_to([P, ST, E]), ALU.is_ge))
                step(dve.tensor_reduce(tile_expert_f[:, :], tile_ge[:, :, :], AX_X, ALU.add))
                dve.tensor_scalar(tile_expert[:, 1:ST + 1], tile_expert_f[:, :], float(E - 1), None, ALU.min).then_inc(experts_ready, 1)
                dve.wait_ge(experts_ready, k + 1)

            def attention():
                def rest(item):
                    b, z, c = item // 4, item // 2 % 2, item % 2
                    dve.wait_ge(part0_ready, item + 1)
                    if item >= 2:
                        dve.wait_ge(parts_ready, item - 1)
                    dve.tensor_tensor(qk_r[item % 2], qk_f[item % 2], qk_split[z][:, 0, 512 * c:512 * (c + 1)], ALU.subtract).then_inc(rest_ready, 1)

                def last_part(item):
                    b, z, c = item // 4, item // 2 % 2, item % 2
                    dve.wait_ge(part1_ready, item + 1)
                    dve.tensor_tensor(qk_split[z][:, 2, 512 * c:512 * (c + 1)], qk_r[item % 2], qk_split[z][:, 1, 512 * c:512 * (c + 1)], ALU.subtract).then_inc(parts_ready, 1)
                for slot_no in range(3):
                    ins = dve.memset(QK[64:96, slot_no, 1, :, :], 1.0)
                ins.then_inc(ones_set, 1)
                rest(0)
                for item in range(4 * BATCH):
                    if item + 1 < 4 * BATCH:
                        rest(item + 1)
                    last_part(item)
                for c in range(4):
                    b = c // 2
                    dve.wait_ge(v_done, c + 1)
                    dve.tensor_tensor(V[:, b * HG:(b + 1) * HG, 4 * (c % 2):4 * (c % 2) + 4, :].rearrange("p g i f -> p i g f"),
                                      PB[c].rearrange("p (i g f) -> p i g f", i=4, g=HG),
                                      b_v[:, :].rearrange("p (g f) -> p g f", g=HG).unsqueeze(1).broadcast_to([P, 4, HG, HG * HD]), ALU.add).then_inc(v_kept, 1)

                def maxima(g, half, u):
                    dve.wait_ge(turn_used, u + 1)
                    heads = slice(2 * half, 2 * half + 2)
                    base = g.n * 8 + 4 * half

                    def link(ins, n):
                        ins.then_inc(max_step, 1)
                        dve.wait_ge(max_step, base + n)
                    for i, (a, z) in ROW_MAXIMA.items():
                        ins = dve.tensor_reduce(neg_max[half][:, :, i], block_max[:, heads, a:z], AX_X, ALU.max, negate=True)
                    link(ins, 1)
                    link(dve.tensor_copy(neg_parts[half][:, 0], neg_max[half][:, :, :]), 2)
                    link(dve.tensor_tensor(neg_rest[half][:, :, :], neg_max[half][:, :, :], neg_parts[half][:, 0], ALU.subtract), 3)
                    link(dve.tensor_copy(neg_parts[half][:, 1], neg_rest[half][:, :, :]), 4)
                    dve.tensor_tensor(neg_parts[half][:, 2], neg_rest[half][:, :, :], neg_parts[half][:, 1], ALU.subtract).then_inc(max_parts_ready, 1)

                def use_turn(u, g, what):
                    bank = turn_bank[parity[0]]
                    parity[0] = 1 - parity[0]
                    dve.wait_ge(turn_done, u + 1)
                    if what[0] == "out":
                        half = what[1]
                        got = bank.rearrange("p (i h f) -> p i h f", i=4, h=HG)
                        dve.reciprocal(inv_sum[half][:, :, :], got[:, :, :, HD]).then_inc(sums_inverted, 1)
                        dve.wait_ge(sums_inverted, (g.n - 1) * 2 + (half + 1))
                        n = g.n - 1
                        dve.tensor_tensor(attn.rearrange("p (b i f) -> p b i f", b=BATCH, i=KB)[:, bass.ds(n // HG, 1), 4 * half:4 * half + 4, bass.ds(n % HG * (HG * HD), HG * HD)]
                                          .rearrange("p b i (h d) -> p (b i) h d", h=HG), got[:, :, :, 0:HD],
                                          inv_sum[half][:, :, :].unsqueeze(3).broadcast_to([P, 4, HG, HD]), ALU.mult).then_inc(turn_used, 1)
                    elif what[0] == "rows":
                        h, chunk = what[1:]
                        dve.tensor_reduce(block_max[:, h, 4 * chunk:4 * chunk + 4], bank.rearrange("p (j k) -> p j k", k=P), AX_X, ALU.max).then_inc(turn_used, 1)
                        if h % 2 == 1 and chunk == RC - 1:
                            maxima(g.plus(1), h // 2, u)
                    else:
                        half = what[1]
                        dve.wait_ge(max_sent[half], (g.n + 1) * 16)
                        dve.tensor_copy(neg_rows[half][:, :], bank.bitcast(BF16)[0:PARTS * 2 * KB, 0:P]).then_inc(turn_used, 1)

                parity = [0]
                before = Group(-1, 2, -1)
                for u, what in enumerate(PRO_TURNS):
                    use_turn(u, before, what)

                def steps(g, first, last):
                    u = 0
                    for t in range(CH):
                        for what in turns_at(t, first, last):
                            use_turn((len(PRO_TURNS) if first else turns_before(g.n)) + u, g, what)
                            u += 1
                group_pipeline(dve, steps)
                for half in range(2):
                    use_turn(turns_before(NG - 1) + 2 + half, Group(NG, 0, 0), ("out", half))
                dve.wait_ge(bias_added, 1)
                for c in range(4):
                    dve.wait_ge(proj_done, c + 1)
                    bank = (6, 7, 0, 1)[c]
                    dve.tensor_tensor(X[:, 4 * c:4 * c + 4, :], X[:, 4 * c:4 * c + 4, :], PB[bank].rearrange("p (t d) -> p t d", t=4), ALU.add).then_inc(attended, 1)
                dve.wait_ge(attended, 4)

            def ffn(k):
                B = k * ST
                route(k)
                if k == 0:
                    dve.wait_ge(w1_loaded, 16)

                def stage(q, m, first, e):
                    s, par = q * 4 + m, m % 2
                    if first is None or first >= 2:
                        dve.wait_ge(up_done, s + (B - 1))
                    dve.tensor_copy(W1S[par][:, :], W1[:, bass.ds(e * HID, HID)]).then_inc(w1_staged, 1)

                def bias(q, m, first, e):
                    s, par = q * 4 + m, m % 2
                    dve.wait_ge(up_done, s + (B + 1))
                    if first is None or first >= 2:
                        dve.wait_ge(gelu_done, s + (B - 1))
                    dve.tensor_tensor(HB[par][:, :].rearrange("p (c q) -> p c q", c=HC), PB[2 + par][:, :].rearrange("p (c q) -> p c q", c=HC),
                                      b1_cols[:, bass.ds(e * HC, HC)].unsqueeze(2).broadcast_to([P, HC, P]), ALU.add).then_inc(up_biased, 1)

                def finish(q, m, first, e):
                    s, par = q * 4 + m, m % 2
                    dve.wait_ge(down_done, s + (B + 1))
                    if first is None or first >= 2:
                        dve.wait_ge(y_sent[par], sent(k, q, m))
                    dve.tensor_tensor(YB[par][:, :], PB[4 + par][:, 0:D], b2_all[:, bass.ds(e * D, D)], ALU.add).then_inc(y_ready, 1)

                def steps(q, m, first, last, experts):
                    if last != ST - 1:
                        stage(*after(q, m, 1), None if first is None else first + 1, experts[m + 2])
                    bias(q, m, first, experts[m + 1])
                    if first != 0:
                        finish(*after(q, m, -1), None if first is None else first - 1, experts[m])
                    if last == ST - 1:
                        finish(q, m, None, experts[m + 1])
                stage(0, 0, 0, experts_of(dve, dve_experts)(0)[1])
                tile_pipeline(dve, steps, experts_of(dve, dve_experts))
                dve.wait_ge(y_back, 16 * (k + 1))
                for t in range(NT):
                    ins = dve.scalar_tensor_tensor(out=X[:, t, :], in0=YT[:, t, :], scalar=half_score[:, t:t + 1], in1=X[:, t, :], op0=ALU.mult, op1=ALU.add)
                ins.then_inc(result_ready, 1)
                dve.wait_ge(result_ready, k + 1)

            dve.memset(tile_expert[:, 0:1], 0)
            dve.memset(tile_expert[:, ST + 1:ST + 3], 0)
            ones_e = sb("ones_e", [P, E])
            ident_ones = ones_e[:, :]
            step(dve.memset(ones_e[:, :], 1.0))
            dve.wait_ge(small_loaded, 144)
            step(dve.tensor_tensor(wg_sq[:, :], wg_sb[:, :], wg_sb[:, :], ALU.mult))
            step(dve.tensor_reduce(wg_norm[:, 2:3], wg_sq[:, :], AX_X, ALU.add))
            dve.tensor_scalar(wg_norm[:, 0:1], wg_norm[:, 2:3], NORM_EPS * NORM_EPS, None, ALU.max).then_inc(norm_var, 1)
            dve.wait_ge(norm_std, 1)
            dve.wait_ge(norm_var, 1)
            refine_rsqrt(wg_norm[:, 3:4], wg_norm[:, 0:1], wg_norm[:, 1:2], wg_norm[:, 4:5], wg_norm[:, 5:6])
            dve.tensor_scalar(wg_unit[:, :], wg_sb[:, :], wg_norm[:, 3:4], None, ALU.mult).then_inc(wgu_t_done, 1)
            dve.wait_ge(gate_w_done, 1)
            dve.tensor_copy(wg_unit_t[:, :], PB[6][0:G, 0:E]).then_inc(wgu_t_done, 1)
            dve.wait_ge(gate_w_done, 2)
            dve.tensor_copy(gate_w[:, :], PB[7][:, 0:E]).then_inc(wgu_t_done, 1)
            dve.wait_ge(b1_t_done, 1)
            dve.tensor_copy(b1_cols[:, :], PB[5][:, 0:E * HC])
            dve.wait_ge(attn_w_done, 1)
            dve.tensor_copy(w_attn_t[:, :], PB[4][:, 0:3 * D])
            dve.tensor_copy(b_attn_cols[:, :], PB[5][:, 64:67]).then_inc(attn_w_kept, 1)
            dve.tensor_copy(w_proj_t[:, :], PB[4][:, 3 * D:4 * D]).then_inc(attn_w_kept, 1)
            norm(0, 2)
            ffn(0)
            norm(1, 3)
            attention()
            norm(2, 4)
            ffn(1)


_INS = ['L0_attn_hidden_states', 'L0_attn_w_attn', 'L0_attn_b_attn', 'L0_attn_w_proj', 'L0_attn_b_proj', 'L0_ffn_wg_red',
        'L0_ffn_wg', 'L0_ffn_w1', 'L0_ffn_b1', 'L0_ffn_w2', 'L0_ffn_b2']


_OUTS = [((2, 1024, 128), 'float32')]


def kernel(**inputs):
    import numpy as _np
    import concourse.bacc as _bacc
    from concourse import mybir as _mybir
    from concourse.bass_utils import run_bass_kernel_spmd as _run

    nc = _bacc.Bacc("TRN2", target_bir_lowering=False, num_devices=1)
    arrays, args = {}, []
    for name in _INS:
        a = _np.ascontiguousarray(inputs[name])
        arrays[f"in_{name}_dram"] = a
        args.append(nc.dram_tensor(f"in_{name}_dram", a.shape, _mybir.dt.from_np(a.dtype), kind="ExternalInput").ap())
    for i, (shape, dtype) in enumerate(_OUTS):
        dt = _mybir.dt.from_np(_np.dtype(dtype))
        args.append(nc.dram_tensor(f"out_{i}_dram", shape, dt, kind="ExternalOutput").ap())
    macaron_kernel(nc, *args)
    r = _run(nc, [arrays], core_ids=[0])
    return r.results[0]["out_0_dram"]
```

```python
from contextlib import ExitStack

import concourse.bass as bass
from concourse import mybir

F32 = mybir.dt.float32
BF16 = mybir.dt.bfloat16
I32 = mybir.dt.int32
ALU = mybir.AluOpType
ACT = mybir.ActivationFunctionType
AX_X = mybir.AxisListType.X

P = 128


def macaron_kernel(nc, x, w_attn, b_attn, w_proj, b_proj, wg_red, wg, w1, b1, w2, b2, out):
    BATCH, SEQ, D = x.shape
    TOK = BATCH * SEQ
    NT = TOK // P
    E, G = wg.shape
    HID = w1.shape[2]
    HC = HID // P
    ST = NT + E - 1
    ROW = D + 4
    LN_EPS, NORM_EPS = 1e-5, 1e-4
    H, HD = 16, D // 16
    HG = 4
    NG = BATCH * H // HG
    KB = SEQ // P
    PARTS = 3
    TERMS = PARTS * PARTS * HD
    SCALE = float(HD) ** -0.5
    MASKED = -1.0e30
    LARGE = 3.4e38
    assert KB == 8 and NG == 8 and HD == 8
    assert D == P and HC * P == HID and ST % 2 == 1

    x_rows = x.rearrange("b (t p) d -> b p t d", p=P)
    out_rows = out.rearrange("b (t p) d -> b p t d", p=P)
    routed = [nc.dram_tensor(f"routed{k}", (ST * P, ROW), F32, kind="Internal").ap() for k in range(2)]
    expert_out = [nc.dram_tensor(f"expert_out{k}", (TOK + ST * P, D), F32, kind="Internal").ap() for k in range(2)]

    q_parts = nc.dram_tensor("q_parts", (NG * HG, PARTS * HD, SEQ), BF16, kind="Internal").ap()
    k_parts = nc.dram_tensor("k_parts", (NG * HG, (2 * PARTS - 1) * HD, SEQ), BF16, kind="Internal").ap()

    ROW_CHUNKS = [[(7, 0, 512, 0)], [(7, 512, 512, 0)], [(6, 0, 512, 0)], [(6, 512, 384, 0), (0, 0, 128, 384)],
                  [(5, 0, 512, 0)], [(5, 512, 256, 0), (1, 0, 256, 256)], [(4, 0, 512, 0)],
                  [(4, 512, 128, 0), (2, 0, 384, 128)], [(3, 0, 512, 0)]]
    ROW_MAXIMA = {7: (0, 8), 6: (8, 15), 0: (15, 16), 5: (16, 22), 1: (22, 24), 4: (24, 29), 2: (29, 32), 3: (32, 36)}
    RC = len(ROW_CHUNKS)

    def key_chunk(t):
        if t >= 16:
            return [(2 * (t - 16) + e, 4, 512 * e - 512) for e in range(2)]
        j = t // 4
        return [(t % 4, j, -128 * j)] + ([(t % 4, 8 - j, 0)] if j else [])
    CH = 18
    PIECES = [(0, 0, 256), (0, 256, 256), (0, 512, 256), (0, 768, 256),
              (1, 128, 384), (1, 512, 256), (1, 768, 256), (7, 896, 128),
              (2, 256, 256), (2, 512, 256), (2, 768, 256), (6, 768, 256),
              (3, 384, 128), (3, 512, 256), (3, 768, 256), (5, 640, 384),
              (4, 512, 256), (4, 768, 256)]
    LAG = 5
    HALF_DONE = (13, 18)
    PROBS = 9

    def last_piece(t):
        return CH - 1 if t >= 16 else 4 * (t // 4) + 3

    ROW_TURNS = [("rows", k // RC, k % RC) for k in range(HG * RC)]
    OUT_AT, MAXIMA_AT = (4, 20), (32, 2)
    ROWS_UNTIL = 50

    def turns_at(place, first=False, last=False):
        out = [("maxima", 1)] if place == MAXIMA_AT[1] and not first else []
        out += [("out", h) for h in range(2) if OUT_AT[h] == place and not first]
        if not last:
            out += [r for k, r in enumerate(ROW_TURNS) if k * ROWS_UNTIL // len(ROW_TURNS) == place]
            out += [("maxima", 0)] if place == MAXIMA_AT[0] else []
        return out
    MIDDLE_TURNS = [turn for place in range(3 * CH) for turn in turns_at(place)]
    PRO_TURNS = ROW_TURNS[:18] + ROW_TURNS[18:20] + [("maxima", 0)] + ROW_TURNS[20:] + [("maxima", 1)]
    GT = len(MIDDLE_TURNS)
    TB = 3

    def turns_before(g):
        return g * GT + (len(PRO_TURNS) + len(ROW_TURNS) + 1 - GT)

    class Group:
        def __init__(self, n, slot, turn):
            self.n, self.slot, self.turn = n, slot, turn

        def plus(self, d):
            return Group(self.n + d, (self.slot + d) % 3, self.turn + (self.slot + d) // 3)

    with ExitStack() as ctx:
        def sb(name, shape, dt=F32):
            return ctx.enter_context(nc.sbuf_tensor(name, shape, dt))

        def sem(name):
            return ctx.enter_context(nc.semaphore(name))

        ident = sb("ident", [P, P])
        ones_bf = sb("ones_bf", [P, P], BF16)
        before_bf = sb("before_bf", [P, P], BF16)
        rank_weight = sb("rank_weight", [P, E])
        tile_starts = sb("tile_starts", [P, E, NT])
        slot_tile_no = sb("slot_tile_no", [P, ST, E])
        blank_all = sb("blank_all", [P, max(ST * ROW, PARTS * SEQ)])
        blank = blank_all[:, 0:ST * ROW].rearrange("p (s r) -> p s r", r=ROW)

        W1 = sb("W1", [P, E * HID])
        W2 = sb("W2", [P, E * HC * D])
        b1_rows = sb("b1_rows", [E * HC, P])
        b1_cols = sb("b1_cols", [P, E * HC])
        b2_all = sb("b2_all", [P, E * D])
        wg_red_sb = sb("wg_red_sb", [G, D])
        wg_sb = sb("wg_sb", [E, G])
        wg_sq = sb("wg_sq", [E, G])
        wg_norm = sb("wg_norm", [E, 8])
        wg_unit = sb("wg_unit", [E, G])
        wg_unit_t = sb("wg_unit_t", [G, E])
        gate_w = sb("gate_w", [P, E])

        X = sb("X", [P, NT, D])
        XR = sb("XR", [P, NT, ROW])
        XT = sb("XT", [P, TOK])
        YT = sb("YT", [P, NT, D])
        w_attn_sb = sb("w_attn_sb", [P, 3, D])
        w_proj_sb = sb("w_proj_sb", [P, D])
        w_attn_t = sb("w_attn_t", [P, 3 * D])
        w_proj_t = sb("w_proj_t", [P, D])
        b_attn_rows = sb("b_attn_rows", [3, D])
        b_attn_cols = sb("b_attn_cols", [P, 3])
        b_v = sb("b_v", [P, D])
        b_p = sb("b_p", [P, D])
        ident_bf = sb("ident_bf", [P, P], BF16)
        row_mask = sb("row_mask", [P, P], BF16)
        key_mask = sb("key_mask", [P, P], BF16)
        QK = sb("QK", [P, 3, 2, HG, SEQ], BF16)
        probs = sb("probs", [P, PROBS, SEQ])
        V = sb("V", [P, NG, KB, HG * HD])
        VS = sb("VS", [P, 3, KB, HG, 32])
        block_max = sb("block_max", [P, HG, 4 * RC])
        zeros = sb("zeros", [P, 2, KB])
        restart = sb("restart", [P, 2 * 4 * RC])
        running_max = [sb(f"running_max{i}", [P, 2 * 4 * RC]) for i in range(2)]
        row_max = [sb(f"row_max{i}", [P, 2, KB]) for i in range(2)]
        max_rest = [sb(f"max_rest{i}", [P, 2, KB]) for i in range(2)]
        max_parts_all = [sb(f"max_parts{i}", [P, P], BF16) for i in range(2)]
        max_parts = [a[:, 0:PARTS * 2 * KB].rearrange("p (a h i) -> p a h i", a=PARTS, h=2) for a in max_parts_all]
        max_rows = [sb(f"max_rows{i}", [PARTS * 2 * KB, P], BF16) for i in range(2)]
        inv_sum = [sb(f"inv_sum{i}", [P, 4, HG]) for i in range(2)]
        stats = sb("stats", [P, NT, 6])
        mean_var = sb("mean_var", [P, NT, 2])
        var_eps = sb("var_eps", [P, NT])
        std = sb("std", [P, NT])
        rstd = sb("rstd", [P, NT])
        nt_a = sb("nt_a", [P, NT])
        nt_b = sb("nt_b", [P, NT])

        gt = [sb(f"gt{i}", [P, NT, E]) for i in range(4)]
        gmax = sb("gmax", [P, NT])
        gsum = sb("gsum", [P, NT])
        half_score = sb("half_score", [P, NT])
        onehot = sb("onehot", [P, NT, E], BF16)
        cum = [sb(f"cum{i}", [P, NT + NT // 2, E]) for i in range(2)]
        etiles = sb("etiles", [P, E])
        etiles_end = sb("etiles_end", [P, E])
        ebase = sb("ebase", [P, E])
        starts_gt = sb("starts_gt", [P, E, NT])
        slot_f = sb("slot_f", [P, NT])
        slot = sb("slot", [P, NT], I32)
        tile_ge = sb("tile_ge", [P, ST, E])
        tile_expert_f = sb("tile_expert_f", [P, ST])
        tile_expert = sb("tile_expert", [P, ST + 3], I32)

        shared = probs[:, :, :].rearrange("p c q -> p (c q)")
        taken = [0]

        def of_shared(width):
            taken[0] += width
            return shared[:, taken[0] - width:taken[0]]
        XS = [of_shared(ROW) for i in range(4)]
        XST = [of_shared(P) for i in range(2)]
        W1S = [of_shared(HID) for i in range(2)]
        HB = [of_shared(HID) for i in range(2)]
        HT = [of_shared(HID) for i in range(2)]
        YB = [of_shared(D) for i in range(2)]
        token_nos = sb("token_nos", [P, ST], I32)
        token_no = [sb(f"token_no{i}", [P, 1], I32) for i in range(2)]

        qk_f = [YT[:, 8 * i:8 * i + 4, :].rearrange("p a d -> p (a d)") for i in range(2)]
        qk_r = [YT[:, 8 * i + 4:8 * i + 8, :].rearrange("p a d -> p (a d)") for i in range(2)]
        blank_bf = blank_all[:, :].bitcast(BF16)
        qk_split = [blank_bf[:, 3072 * z:3072 * (z + 1)].rearrange("p (a t) -> p a t", a=PARTS) for z in range(2)]
        attn = YT[:, :, :].rearrange("p t d -> p (t d)")
        out_t = XT[:, 0:SEQ]
        attn_t = XT[:, :]

        PS = ctx.enter_context(nc.psum_tensor("PS", [P, 8 * 512], F32))
        PB = [PS[:, 512 * i:512 * (i + 1)] for i in range(8)]
        turn_bank, key_bank = PB[0:TB], PB[3:6]
        out_acc = PS[:, 3072:4096]

        x_loaded = [sem(f"x_loaded{b}") for b in range(BATCH)]
        small_loaded = sem("small_loaded")
        w1_loaded, w2_loaded = sem("w1_loaded"), sem("w2_loaded")
        consts_made = sem("consts_made")
        pool_step = sem("pool_step")
        dve_step = sem("dve_step")
        blanked = [sem(f"blanked{k}") for k in range(2)]
        wgu_t_done, gate_w_done, b1_t_done = sem("wgu_t_done"), sem("gate_w_done"), sem("b1_t_done")
        norm_var, norm_std = sem("norm_var"), sem("norm_std")
        norm_rows = sem("norm_rows")
        rows_turned, turned_kept = sem("rows_turned"), sem("turned_kept")
        logits_done, logits_less_max, gates_exp = sem("logits_done"), sem("logits_less_max"), sem("gates_exp")
        onehot_ready, counts_done = sem("onehot_ready"), sem("counts_done")
        slots_ready, experts_ready = sem("slots_ready"), sem("experts_ready")
        rows_routed = sem("rows_routed")
        xs_loaded = [sem(f"xs_loaded{i}") for i in range(4)]
        xs_turned, xst_kept = sem("xs_turned"), sem("xst_kept")
        w1_staged = sem("w1_staged")
        up_done, up_biased, gelu_done = sem("up_done"), sem("up_biased"), sem("gelu_done")
        down_done, y_ready = sem("down_done"), sem("y_ready")
        token_no_kept, token_no_at_pool = sem("token_no_kept"), sem("token_no_at_pool")
        y_sent = [sem(f"y_sent{i}") for i in range(2)]
        y_back = sem("y_back")
        attn_w_done, attn_w_kept = sem("attn_w_done"), sem("attn_w_kept")
        qk_done, qk_kept, part0_ready, rest_ready, part1_ready = (sem(n) for n in ("qk_done", "qk_kept", "part0_ready", "rest_ready", "part1_ready"))
        parts_ready, parts_sent = sem("parts_ready"), [sem(f"parts_sent{z}") for z in range(2)]
        v_done, v_kept, v_staged = sem("v_done"), sem("v_kept"), sem("v_staged")
        qk_loaded = [sem(f"qk_loaded{i}") for i in range(3)]
        ones_set = sem("ones_set")
        turn_done, turn_used = sem("turn_done"), sem("turn_used")
        maxima_found, max_step, max_parts_ready = sem("maxima_found"), sem("max_step"), sem("max_parts_ready")
        max_sent = [sem(f"max_sent{h}") for h in range(2)]
        scores_done, probs_ready, pieces_done, out_kept, sums_inverted = (sem(n) for n in ("scores_done", "probs_ready", "pieces_done", "out_kept", "sums_inverted"))
        attn_turned, attn_kept, proj_done = sem("attn_turned"), sem("attn_kept"), sem("proj_done")
        bias_added, attended = sem("bias_added"), sem("attended")
        result_ready, stored = sem("result_ready"), sem("stored")

        def loaded(k, q, m):
            return q * 16 + 16 * (k * ((ST - 1 - m) // 4 + 1) + 1)

        def sent(k, q, m, more=0):
            return q * 32 + 16 * (k * ((ST + 1 - m % 2) // 2) + m // 2 + more)

        def after(q, m, d):
            return q + (m + d) // 4, (m + d) % 4

        def experts_of(engine, registers):
            def load(q):
                engine.load(registers, tile_expert[0:1, bass.ds(q * 4, 6)])
                return [engine.snap(r, min_val=0, max_val=E - 1) for r in registers]
            return load

        def tile_pipeline(engine, steps, begin=lambda q: None):
            at_q = begin(0)
            for m in range(4):
                steps(0, m, m, None, at_q)
            with engine.Fori(1, (ST - 3) // 4) as q:
                at_q = begin(q)
                for m in range(4):
                    steps(q, m, None, None, at_q)
            at_q = begin((ST - 3) // 4)
            for m in range(3):
                steps((ST - 3) // 4, m, None, ST - 3 + m, at_q)

        def max_turn(g, half):
            if isinstance(g.n, int) and g.n == 0:
                return PRO_TURNS.index(("maxima", half)) + 1
            if isinstance(g.n, int) and g.n == NG - 1 and half:
                return turns_before(g.n) + 1
            return turns_before(g.n - (1 - half)) + (MIDDLE_TURNS.index(("maxima", half)) + 1)

        def out_turn(g, half):
            return turns_before(g.n + 1) + (MIDDLE_TURNS.index(("out", half)) + 1)

        def group_pipeline(engine, steps):
            steps(Group(0, 0, 0), True, False)
            with engine.Fori(0, (NG - 2) // 3) as i:
                for j in range(3):
                    steps(Group(i * 3 + (1 + j), (1 + j) % 3, i + (1 + j) // 3), False, False)
            steps(Group(NG - 1, (NG - 1) % 3, (NG - 1) // 3), False, True)

        block = ctx.enter_context(nc.Block())

        @block.sync
        def _(sp):
            for b in range(BATCH):
                sp.dma_start(X[:, b * NT // BATCH:(b + 1) * NT // BATCH, :], x_rows[b]).then_inc(x_loaded[b], 16)
            sp.dma_start(wg_red_sb[:, :], wg_red).then_inc(small_loaded, 16)
            sp.dma_start(wg_sb[:, :], wg).then_inc(small_loaded, 16)
            sp.dma_start(b1_rows[:, :], b1.rearrange("e (c p) -> (e c) p", p=P)).then_inc(small_loaded, 16)
            sp.dma_start(b2_all[:, :], b2.rearrange("(o e) d -> o (e d)", o=1).broadcast_to([P, E * D])).then_inc(small_loaded, 16)
            sp.dma_start(w_attn_sb[:, :, :], w_attn.rearrange("(a p) d -> p a d", p=P)).then_inc(small_loaded, 16)
            sp.dma_start(w_proj_sb[:, :], w_proj).then_inc(small_loaded, 16)
            sp.dma_start(b_attn_rows[:, :], b_attn.rearrange("(a d) -> a d", a=3)).then_inc(small_loaded, 16)
            sp.dma_start(b_v[:, :], b_attn[2 * D:3 * D].rearrange("(o d) -> o d", o=1).broadcast_to([P, D])).then_inc(small_loaded, 16)
            sp.dma_start(b_p[:, :], b_proj.rearrange("(o d) -> o d", o=1).broadcast_to([P, D])).then_inc(small_loaded, 16)
            sp.wait_ge(consts_made, 1)
            for k in range(2):
                sp.dma_start(routed[k].rearrange("(s p) r -> p s r", p=P), blank[:, :, :]).then_inc(blanked[k], 16)
            sp.dma_start(W1[:, :].rearrange("p (e h) -> p e h", e=E), w1.rearrange("e p h -> p e h")).then_inc(w1_loaded, 16)
            sp.dma_start(W2[:, :].rearrange("p (e c d) -> p e c d", e=E, c=HC), w2.rearrange("e (c p) d -> p e c d", p=P)).then_inc(w2_loaded, 16)

            def ffn(k):
                B = k * ST

                def load(q, m, first, last, _):
                    s = q * 4 + m
                    if first is None:
                        sp.wait_ge(xs_turned, s + (B - 3))
                        sp.wait_ge(token_no_kept, s + (B - 3))
                    sp.dma_start(XS[m][:, :], routed[k][bass.ds(s * P, P), :]).then_inc(xs_loaded[m], 16)
                sp.wait_ge(rows_routed, 16 * NT * (k + 1))
                tile_pipeline(sp, load)
                for par in range(2):
                    sp.wait_ge(y_sent[par], 16 * (k + 1) * ((ST + 1 - par) // 2))
                sp.dma_start(YT[:, :, :], expert_out[k][0:TOK, :].rearrange("(t p) d -> p t d", p=P)).then_inc(y_back, 16)

            def attention():
                def send_parts(b):
                    for z, parts in ((0, q_parts), (1, k_parts)):
                        for block_no in range(PARTS if z == 0 else 2 * PARTS - 1):
                            if block_no < PARTS:
                                sp.wait_ge(parts_ready, 4 * b + 2 * z + 2)
                            sp.dma_start(parts[b * H:(b + 1) * H, block_no * HD:(block_no + 1) * HD, :],
                                         qk_split[z][:, block_no % PARTS, :]).then_inc(parts_sent[z], 16)

                def load(g):
                    for r in range(PARTS):
                        sp.dma_start(QK[24 * r:24 * r + 24, g.slot, 0, :, :],
                                     q_parts[bass.ds(g.n * HG, HG), :, :].rearrange("h r t -> r h t")).then_inc(qk_loaded[g.slot], 16)
                        sp.dma_start(QK[24 * r:24 * r + 24, g.slot, 1, :, :],
                                     k_parts[bass.ds(g.n * HG, HG), 8 * r:8 * r + 24, :].rearrange("h r t -> r h t")).then_inc(qk_loaded[g.slot], 16)

                def send_max(g, half):
                    sp.wait_ge(turn_used, max_turn(g, half))
                    sp.dma_start(QK[TERMS:TERMS + PARTS, g.slot, 0, 2 * half:2 * half + 2, :], max_rows[half][:, :]).then_inc(max_sent[half], 16)
                def wait_sent(b):
                    sp.wait_ge(parts_sent[0], 16 * PARTS * (b + 1))
                    sp.wait_ge(parts_sent[1], 16 * (2 * PARTS - 1) * (b + 1))
                send_parts(0)
                sp.wait_ge(ones_set, 3)
                wait_sent(0)
                load(Group(0, 0, 0))
                send_parts(1)
                load(Group(1, 1, 0))
                wait_sent(1)
                for half in range(2):
                    send_max(Group(0, 0, 0), half)
                with sp.Fori(0, (NG - 2) // 3) as i:
                    for j in range(3):
                        g = Group(i * 3 + j, j, i)
                        sp.wait_ge(scores_done, g.n * (2 * CH) + 1)
                        load(g.plus(2))
                        for half in range(2):
                            send_max(g.plus(1), half)
                for half in range(2):
                    send_max(Group(NG - 1, (NG - 1) % 3, (NG - 1) // 3), half)
            ffn(0)
            attention()
            ffn(1)
            sp.wait_ge(result_ready, 2)
            for b in range(BATCH):
                sp.dma_start(out_rows[b], X[:, b * NT // BATCH:(b + 1) * NT // BATCH, :]).then_inc(stored, 16)
            sp.wait_ge(stored, 16 * BATCH)

        @block.gpsimd
        def _(pool):
            n = [0]

            def step(ins):
                n[0] += 1
                ins.then_inc(pool_step, 1)
                pool.wait_ge(pool_step, n[0])

            step(pool.memset(blank[:, :, :], 0.0))
            step(pool.iota(blank[:, :, D:D + 1].bitcast(I32).rearrange("p s o -> p (s o)"), [[P, ST]], base=TOK, channel_multiplier=1))
            pool.memset(ones_bf[:, :], 1.0).then_inc(consts_made, 1)
            step(pool.memset(ident[:, :], 0.0))
            step(pool.affine_select(out=ident[:, :], in_=ident[:, :], compare_op=ALU.not_equal, fill=1.0, base=0, pattern=[[-1, P]], channel_multiplier=1))
            step(pool.memset(before_bf[:, :], 1.0))
            step(pool.affine_select(out=before_bf[:, :], in_=before_bf[:, :], compare_op=ALU.is_gt, fill=0.0, base=0, pattern=[[1, P]], channel_multiplier=-1))
            step(pool.memset(row_mask[:, :], 0.0))
            step(pool.affine_select(out=row_mask[:, :], in_=row_mask[:, :], compare_op=ALU.is_ge, fill=MASKED, base=0, pattern=[[-1, P]], channel_multiplier=1))
            step(pool.memset(key_mask[:, :], 0.0))
            step(pool.affine_select(out=key_mask[:, :], in_=key_mask[:, :], compare_op=ALU.is_ge, fill=MASKED, base=0, pattern=[[1, P]], channel_multiplier=-1))
            step(pool.tensor_copy(ident_bf[:, :], ident[:, :]))
            step(pool.memset(VS[:, :, :, :, :], 0.0))
            for half in range(2):
                step(pool.memset(max_parts_all[half][:, :], 0.0))
            step(pool.memset(VS[:, :, :, :, HD:HD + 1], 1.0))
            step(pool.memset(zeros[:, :, :], 0.0))
            step(pool.memset(restart[:, :], LARGE))
            for a, z in ROW_MAXIMA.values():
                ins = pool.memset(restart[:, :].rearrange("p (h b) -> p h b", h=2)[:, :, a:a + 1], -LARGE)
            step(ins)
            step(pool.iota(rank_weight[:, :], [[-1, E]], base=E, channel_multiplier=0, allow_small_or_imprecise_dtypes=True))
            step(pool.iota(tile_starts[:, :, :], [[0, E], [P, NT]], base=0, channel_multiplier=0, allow_small_or_imprecise_dtypes=True))
            step(pool.iota(slot_tile_no[:, :, :], [[1, ST], [0, E]], base=0, channel_multiplier=0, allow_small_or_imprecise_dtypes=True))
            step(pool.memset(cum[0][:, 0:NT // 2, :], 0.0))
            step(pool.memset(cum[1][:, 0:NT // 2, :], 0.0))
            step(pool.memset(XR[:, :, D:ROW], 0.0))
            pool.iota(XR[:, :, D:D + 1].bitcast(I32).rearrange("p s o -> p (s o)"), [[P, NT]], base=0, channel_multiplier=1).then_inc(consts_made, 1)
            pool.wait_ge(consts_made, 2)
            for slot_no in range(3):
                pool.memset(QK[64:96, slot_no, 1, :, :], -1.0).then_inc(ones_set, 1)
                pool.wait_ge(ones_set, slot_no + 1)

            def ffn(k):
                B = k * ST
                pool.wait_ge(slots_ready, k + 1)
                pool.wait_ge(blanked[k], 16)
                for t in range(NT):
                    pool.indirect_dma_start(routed[k], bass.IndirectOffsetOnAxis(ap=slot[:, t:t + 1], axis=0),
                                            XR[:, t, :], None).then_inc(rows_routed, 16)

                def send(q, m, first, last, _):
                    s, par = q * 4 + m, m % 2
                    pool.wait_ge(token_no_kept, s + (B + 1))
                    if first is None or first >= 2:
                        pool.wait_ge(y_sent[par], sent(k, q, m))
                    pool.tensor_copy(token_no[par][:, :], token_nos[:, bass.ds(s, 1)]).then_inc(token_no_at_pool, 1)
                    pool.wait_ge(slots_ready, k + 1)
                    pool.wait_ge(token_no_at_pool, s + (B + 1))
                    pool.wait_ge(y_ready, s + (B + 1))
                    pool.indirect_dma_start(expert_out[k], bass.IndirectOffsetOnAxis(ap=token_no[par][:, 0:1], axis=0),
                                            YB[par][:, :], None).then_inc(y_sent[par], 16)
                tile_pipeline(pool, send)

            def attention():
                pool.wait_ge(norm_rows, 2 * NT)
                pool.tensor_tensor(X[:, :, :], X[:, :, :], b_p[:, :].unsqueeze(1).broadcast_to([P, NT, D]), ALU.add).then_inc(bias_added, 1)

                def stage(g):
                    pool.tensor_copy(VS[:, g.slot, :, :, 0:HD], V[:, :, :, :].rearrange("p g i f -> p (g i f)")[:, bass.ds(g.n * (KB * HG * HD), KB * HG * HD)]
                                     .rearrange("p (i h d) -> p i h d", i=KB, h=HG)).then_inc(v_staged, 1)
                def split_maxima(g, half):
                    base = g.n * 8 + 4 * half

                    def link(ins, k):
                        ins.then_inc(max_step, 1)
                        pool.wait_ge(max_step, base + k)
                    pool.wait_ge(maxima_found, g.n * 2 + (half + 1))
                    for i, (a, z) in ROW_MAXIMA.items():
                        ins = pool.tensor_tensor(row_max[half][:, :, i:i + 1], running_max[half][:, :].rearrange("p (h b) -> p h b", h=2)[:, :, z - 1:z], zeros[:, :, 0:1], ALU.add)
                    link(ins, 1)
                    link(pool.tensor_tensor(max_parts[half][:, 0], row_max[half][:, :, :], zeros[:, :, :], ALU.add), 2)
                    link(pool.tensor_tensor(max_rest[half][:, :, :], row_max[half][:, :, :], max_parts[half][:, 0], ALU.subtract), 3)
                    link(pool.tensor_tensor(max_parts[half][:, 1], max_rest[half][:, :, :], zeros[:, :, :], ALU.add), 4)
                    pool.tensor_tensor(max_parts[half][:, 2], max_rest[half][:, :, :], max_parts[half][:, 1], ALU.subtract).then_inc(max_parts_ready, 1)
                pool.wait_ge(v_kept, 4)
                stage(Group(0, 0, 0))
                stage(Group(1, 1, 0))
                for half in range(2):
                    split_maxima(Group(0, 0, 0), half)
                with pool.Fori(0, (NG - 2) // 3) as i:
                    for j in range(3):
                        g = Group(i * 3 + j, j, i)
                        pool.wait_ge(v_kept, 4)
                        pool.wait_ge(pieces_done, g.n * CH + 1)
                        stage(g.plus(2))
                        for half in range(2):
                            split_maxima(g.plus(1), half)
                for half in range(2):
                    split_maxima(Group(NG - 1, (NG - 1) % 3, (NG - 1) // 3), half)
            ffn(0)
            attention()
            ffn(1)

        @block.scalar
        def _(act):
            def norm(q):
                act.wait_ge(norm_var, q + 1)
                act.activation(std[:, :], var_eps[:, :], ACT.Sqrt).then_inc(norm_std, 1)

            def keep_rows(q):
                for c in range(4):
                    act.wait_ge(rows_turned, 4 * q + c + 1)
                    act.activation(XT[:, c * 512:(c + 1) * 512], PB[c][:, :], ACT.Copy).then_inc(turned_kept, 1)

            def ffn(k):
                B = k * ST
                keep_rows(2 * k)
                act.wait_ge(logits_less_max, k + 1)
                act.activation(gt[1][:, :, :], gt[0][:, :, :], ACT.Exp).then_inc(gates_exp, 1)

                def keep_turned(q, m, first):
                    s, par = q * 4 + m, m % 2
                    act.wait_ge(xs_turned, s + (B + 1))
                    if first is None or first >= 2:
                        act.wait_ge(up_done, s + (B - 1))
                    act.activation(XST[par][:, :], PB[par][:, 0:P], ACT.Copy).then_inc(xst_kept, 1)
                    act.activation(token_nos[:, bass.ds(s, 1)], XS[m][:, D:D + 1].bitcast(I32), ACT.Copy).then_inc(token_no_kept, 1)

                def gelu(q, m, first):
                    s, par = q * 4 + m, m % 2
                    act.wait_ge(up_biased, s + (B + 1))
                    if first is None or first >= 2:
                        act.wait_ge(down_done, s + (B - 1))
                    act.activation(HT[par][:, :], HB[par][:, :], ACT.Gelu).then_inc(gelu_done, 1)

                def steps(q, m, first, last, experts):
                    if last != ST - 1:
                        keep_turned(*after(q, m, 1), None if first is None else first + 1)
                    gelu(q, m, first)
                keep_turned(0, 0, 0)
                tile_pipeline(act, steps)
            def attention():
                keep_rows(1)
                for item in range(4 * BATCH):
                    b, z, c = item // 4, item // 2 % 2, item % 2
                    act.wait_ge(qk_done, item + 1)
                    if item >= 2:
                        act.wait_ge(rest_ready, item - 1)
                    act.activation(qk_f[item % 2], PB[4 + item % 4], ACT.Identity, bias=b_attn_cols[:, z:z + 1]).then_inc(qk_kept, 1)
                    act.wait_ge(qk_kept, item + 1)
                    if b and c == 0:
                        act.wait_ge(parts_sent[z], 16 * (PARTS if z == 0 else 2 * PARTS - 1))
                    act.activation(qk_split[z][:, 0, 512 * c:512 * (c + 1)], qk_f[item % 2], ACT.Copy).then_inc(part0_ready, 1)

                def keep_out(g, half, final=False):
                    act.wait_ge(pieces_done, g.n * CH + HALF_DONE[half])
                    act.wait_ge(turn_done, turns_before(NG - 1) + half + 2 if final else out_turn(g, half) - GT)
                    act.activation(out_t[:, 512 * half:512 * (half + 1)], out_acc[:, 512 * half:512 * (half + 1)], ACT.Copy).then_inc(out_kept, 1)

                def steps(g, first, last):
                    for t in range(CH):
                        if not first and t == 0:
                            keep_out(g.plus(-1), 0)
                        if not first and t == LAG:
                            keep_out(g.plus(-1), 1)
                        if t >= PROBS:
                            act.wait_ge(pieces_done, g.n * CH + (last_piece(t - PROBS) + 1))
                        elif not first:
                            act.wait_ge(pieces_done, (g.n - 1) * CH + (last_piece(t + PROBS) + 1))
                        for c in range(2):
                            act.wait_ge(scores_done, g.n * (2 * CH) + (2 * t + c + 1))
                            act.activation(probs[:, t % PROBS, 512 * c:512 * (c + 1)], key_bank[(2 * t + c) % 3], ACT.Exp, scale=SCALE).then_inc(probs_ready, 1)
                group_pipeline(act, steps)
                for half in range(2):
                    keep_out(Group(NG - 1, 0, 0), half, True)
                for c in range(4):
                    act.wait_ge(attn_turned, c + 1)
                    act.activation(attn_t[:, 512 * c:512 * (c + 1)], PB[2 + c], ACT.Copy).then_inc(attn_kept, 1)
            act.wait_ge(norm_var, 1)
            act.activation(wg_norm[:, 1:2], wg_norm[:, 0:1], ACT.Sqrt).then_inc(norm_std, 1)
            norm(1)
            ffn(0)
            norm(2)
            attention()
            norm(3)
            ffn(1)

        @block.tensor
        def _(pe):
            pe_experts = [pe.alloc_register(f"pe_expert{j}") for j in range(6)]
            pe.wait_ge(consts_made, 2)
            pe.wait_ge(small_loaded, 144)
            for a in range(3):
                pe.transpose(PB[4][:, a * P:(a + 1) * P], w_attn_sb[:, a, :], ident[:, :])
            pe.transpose(PB[4][:, 3 * P:4 * P], w_proj_sb[:, :], ident[:, :]).then_inc(attn_w_done, 1)
            pe.transpose(PB[5][:, 64:67], b_attn_rows[:, :], ident[0:3, 0:3])
            pe.transpose(PB[5][:, 0:E * HC], b1_rows[:, :], ident[0:E * HC, 0:E * HC]).then_inc(b1_t_done, 1)
            pe.wait_ge(wgu_t_done, 1)
            pe.transpose(PB[6][0:G, 0:E], wg_unit[:, :], ident[0:E, 0:E]).then_inc(gate_w_done, 1)
            pe.wait_ge(wgu_t_done, 2)
            pe.matmul(PB[7][:, 0:E], wg_red_sb[:, :], wg_unit_t[:, :], start=True, stop=True).then_inc(gate_w_done, 1)

            def turn_rows(q):
                for t in range(NT):
                    pe.wait_ge(norm_rows, NT * q + t + 1)
                    mm = pe.transpose(PB[t // 4][:, (t % 4) * P:(t % 4 + 1) * P], XR[:, t, 0:D], ident[:, :])
                    if t % 4 == 3:
                        mm.then_inc(rows_turned, 1)

            def ffn(k):
                B = k * ST
                turn_rows(2 * k)
                pe.wait_ge(wgu_t_done, 3)
                for t in range(NT):
                    if t % 4 == 0:
                        pe.wait_ge(turned_kept, 8 * k + t // 4 + 1)
                    mm = pe.matmul(PB[6][:, t * E:(t + 1) * E], XT[:, t * P:(t + 1) * P], gate_w[:, :], start=True, stop=True)
                mm.then_inc(logits_done, 1)
                pe.wait_ge(onehot_ready, k + 1)
                pe.matmul(PB[7][:, 0:NT * E], before_bf[:, :], onehot[:, :, :].rearrange("p t e -> p (t e)"), start=True, stop=True)
                pe.matmul(PB[7][:, 128:128 + NT * E], ones_bf[:, :], onehot[:, :, :].rearrange("p t e -> p (t e)"), start=True, stop=True).then_inc(counts_done, 1)
                pe.wait_ge(experts_ready, k + 1)
                if k == 0:
                    pe.wait_ge(w2_loaded, 16)

                def turn(q, m, first):
                    s, par = q * 4 + m, m % 2
                    pe.wait_ge(xs_loaded[m], loaded(k, q, m))
                    if first is None or first >= 2:
                        pe.wait_ge(xst_kept, s + (B - 1))
                    pe.transpose(PB[par][:, 0:P], XS[m][:, 0:D], ident[:, :]).then_inc(xs_turned, 1)

                def up(q, m, first):
                    s, par = q * 4 + m, m % 2
                    pe.wait_ge(xst_kept, s + (B + 1))
                    pe.wait_ge(w1_staged, s + (B + 1))
                    if first is None or first >= 2:
                        pe.wait_ge(up_biased, s + (B - 1))
                    for c in range(HC):
                        mm = pe.matmul(PB[2 + par][:, c * P:(c + 1) * P], W1S[par][:, c * P:(c + 1) * P], XST[par][:, :], start=True, stop=True)
                    mm.then_inc(up_done, 1)

                def down(q, m, first, e):
                    s, par = q * 4 + m, m % 2
                    pe.wait_ge(gelu_done, s + (B + 1))
                    if first is None or first >= 2:
                        pe.wait_ge(y_ready, s + (B - 1))
                    for c in range(HC):
                        mm = pe.matmul(PB[4 + par][:, 0:D], HT[par][:, c * P:(c + 1) * P], W2[:, bass.ds(e * HID + c * D, D)], start=(c == 0), stop=(c == HC - 1))
                    mm.then_inc(down_done, 1)

                def steps(q, m, first, last, experts):
                    if last != ST - 1:
                        turn(*after(q, m, 1), None if first is None else first + 1)
                    up(q, m, first)
                    if first != 0:
                        down(*after(q, m, -1), None if first is None else first - 1, experts[m])
                    if last == ST - 1:
                        down(q, m, None, experts[m + 1])
                turn(0, 0, 0)
                tile_pipeline(pe, steps, experts_of(pe, pe_experts))

            def attention():
                turn_rows(1)
                pe.wait_ge(attn_w_kept, 2)
                for item in range(4 * BATCH):
                    b, z, c = item // 4, item // 2 % 2, item % 2
                    pe.wait_ge(turned_kept, 4 + 2 * b + c + 1)
                    if item >= 4:
                        pe.wait_ge(qk_kept, item - 3)
                    pe.matmul(PB[4 + item % 4], w_attn_t[:, z * D:(z + 1) * D], XT[:, SEQ * b + 512 * c:SEQ * b + 512 * (c + 1)], start=True, stop=True).then_inc(qk_done, 1)
                for t in range(NT):
                    mm = pe.matmul(PB[t // 4][:, (t % 4) * P:(t % 4 + 1) * P], XT[:, t * P:(t + 1) * P], w_attn_t[:, 2 * D:3 * D], start=True, stop=True)
                    if t % 4 == 3:
                        mm.then_inc(v_done, 1)

                def take_turn(u, g, what):
                    bank = turn_bank[parity[0]]
                    parity[0] = (parity[0] + 1) % TB
                    if not isinstance(u, int) or u >= TB:
                        pe.wait_ge(turn_used, u - (TB - 1))
                    if what[0] == "out":
                        half = what[1]
                        pe.wait_ge(out_kept, (g.n - 1) * 2 + (half + 1))
                        for i in range(4):
                            mm = pe.transpose(bank[:, i * P:(i + 1) * P], out_t[:, 512 * half + i * P:512 * half + (i + 1) * P], ident[:, :])
                    elif what[0] == "rows":
                        h, chunk = what[1:]
                        g = g.plus(1)
                        if h == 0 and chunk == 0:
                            pe.wait_ge(qk_loaded[g.slot], g.turn * (96) + 96)
                        for n, (i, key, keys, col) in enumerate(ROW_CHUNKS[chunk]):
                            diag = key + keys == (i + 1) * P
                            last = n == len(ROW_CHUNKS[chunk]) - 1
                            mm = pe.matmul(bank[:, col:col + keys], QK[0:TERMS, g.slot, 0, h, i * P:(i + 1) * P], QK[0:TERMS, g.slot, 1, h, key:key + keys],
                                           start=(n == 0), stop=(last and not diag), skip_group_check=True)
                            if diag:
                                mm = pe.matmul(bank[:, col + keys - P:col + keys], ident_bf[:, :], row_mask[:, :], start=False, stop=last, skip_group_check=True)
                    else:
                        half = what[1]
                        pe.wait_ge(max_parts_ready, (g.n if half and g.n is not before.n else g.n + 1) * 2 + (half + 1))
                        mm = pe.transpose(bank.bitcast(BF16)[:, 0:P], max_parts_all[half][:, :], ident_bf[:, :])
                    mm.then_inc(turn_done, 1)

                def scores(g, t, c, first):
                    r = 2 * t + c
                    if t < HG and r % 4 == 0:
                        pe.wait_ge(max_sent[t // 2], g.n * 16 + 16)
                    if r >= 3 or not first:
                        pe.wait_ge(probs_ready, g.n * (2 * CH) + (r - 2))
                    bank = key_bank[r % 3]
                    start = True
                    for h, j, q0 in key_chunk(t):
                        diagonal = q0 + P * j
                        at, end = max(diagonal, 512 * c), min(q0 + SEQ, 512 * (c + 1))
                        if at < end:
                            mm = pe.matmul(bank[:, at - 512 * c:end - 512 * c], QK[0:TERMS + PARTS, g.slot, 1, h, j * P:(j + 1) * P],
                                           QK[0:TERMS + PARTS, g.slot, 0, h, at - q0:end - q0], start=start, stop=False, skip_group_check=True)
                            start = False
                            if at == diagonal:
                                mm = pe.matmul(bank[:, at - 512 * c:at - 512 * c + P], ident_bf[:, :], key_mask[:, :], start=False, stop=True, skip_group_check=True)
                    mm.then_inc(scores_done, 1)

                def piece(g, n, first):
                    j, query, width = PIECES[n]
                    if n == 0:
                        pe.wait_ge(v_staged, g.n + 1)
                    if n in (0, 2) and not first:
                        pe.wait_ge(out_kept, g.n * 2 - 1 + n // 2)
                    pe.wait_ge(probs_ready, g.n * (2 * CH) + 2 * (CH if n >= 16 else 4 * (n // 4) + 4))
                    for h in range(HG):
                        chunk = 16 + h // 2 if n >= 16 else 4 * (n // 4) + h
                        at = query + next(q0 for hh, jj, q0 in key_chunk(chunk) if (hh, jj) == (h, j))
                        mm = pe.matmul(out_acc[32 * h:32 * h + 32, query:query + width], VS[:, g.slot, j, h, :], probs[:, chunk % PROBS, at:at + width],
                                       start=(n in (0, 2)), stop=(n in (12, 17)), skip_group_check=True, tile_position=(0, 32 * h))
                    mm.then_inc(pieces_done, 1)

                parity = [0]
                before = Group(-1, 2, -1)
                pe.wait_ge(v_kept, 4)
                pe.wait_ge(qk_kept, 4 * BATCH)
                for u, what in enumerate(PRO_TURNS):
                    take_turn(u, before, what)

                def steps(g, first, last):
                    u = [0]

                    def turns(place):
                        for what in turns_at(place, first, last):
                            take_turn((len(PRO_TURNS) if first else turns_before(g.n)) + u[0], g, what)
                            u[0] += 1
                    for t in range(CH):
                        for c in range(2):
                            scores(g, t, c, first)
                            turns(3 * t + c)
                        if t >= LAG:
                            piece(g, t - LAG, first)
                        elif not first:
                            piece(g.plus(-1), t - LAG + CH, False)
                        turns(3 * t + 2)
                group_pipeline(pe, steps)
                g = Group(NG - 1, (NG - 1) % 3, (NG - 1) // 3)
                for n in range(CH - LAG, CH):
                    piece(g, n, False)
                for half in range(2):
                    take_turn(turns_before(NG - 1) + 3 + half, g.plus(1), ("out", half))
                pe.wait_ge(turn_used, turns_before(NG - 1) + 5)
                for t in range(NT):
                    mm = pe.transpose(PB[2 + t // 4][:, (t % 4) * P:(t % 4 + 1) * P], attn[:, t * D:(t + 1) * D], ident[:, :])
                    if t % 4 == 3:
                        mm.then_inc(attn_turned, 1)
                for t in range(NT):
                    if t % 4 == 0:
                        pe.wait_ge(attn_kept, t // 4 + 1)
                    bank = (6, 7, 0, 1)[t // 4]
                    mm = pe.matmul(PB[bank][:, (t % 4) * P:(t % 4 + 1) * P], attn_t[:, t * P:(t + 1) * P], w_proj_t[:, :], start=True, stop=True)
                    if t % 4 == 3:
                        mm.then_inc(proj_done, 1)
            ffn(0)
            attention()
            ffn(1)

        @block.vector
        def _(dve):
            n = [0]
            dve_experts = [dve.alloc_register(f"dve_expert{j}") for j in range(6)]

            def step(ins):
                n[0] += 1
                ins.then_inc(dve_step, 1)
                dve.wait_ge(dve_step, n[0])

            def refine_rsqrt(r, v, s, a, b):
                step(dve.reciprocal(r, s))
                step(dve.tensor_tensor(a, r, r, ALU.mult))
                step(dve.tensor_tensor(b, a, v, ALU.mult))
                step(dve.tensor_scalar(a, b, -0.5, 1.5, ALU.mult, ALU.add))
                step(dve.tensor_tensor(r, r, a, ALU.mult))

            def norm(q, var_at):
                for t in range(NT):
                    if q == 0 and t % (NT // BATCH) == 0:
                        dve.wait_ge(x_loaded[t // (NT // BATCH)], 16)
                    ins = dve.bn_stats(stats[:, t, :], X[:, t, :])
                step(ins)
                for t in range(NT):
                    ins = dve.bn_aggr(mean_var[:, t, :], stats[:, t, :])
                step(ins)
                dve.tensor_scalar(var_eps[:, :], mean_var[:, :, 1], LN_EPS, None, ALU.add).then_inc(norm_var, 1)
                dve.wait_ge(norm_std, var_at)
                dve.wait_ge(norm_var, var_at)
                refine_rsqrt(rstd[:, :], var_eps[:, :], std[:, :], nt_a[:, :], nt_b[:, :])
                dve.wait_ge(consts_made, 2)
                for t in range(NT):
                    dve.tensor_scalar(XR[:, t, 0:D], X[:, t, :], mean_var[:, t, 0:1], rstd[:, t:t + 1], ALU.subtract, ALU.mult).then_inc(norm_rows, 1)

            def by_tile(a):
                return a.unsqueeze(2).broadcast_to([P, NT, E])

            def route(k):
                dve.wait_ge(logits_done, k + 1)
                logits = PB[6][:, 0:NT * E].rearrange("p (t e) -> p t e", e=E)
                step(dve.tensor_reduce(gmax[:, :], logits, AX_X, ALU.max))
                dve.tensor_tensor(gt[0][:, :, :], logits, by_tile(gmax[:, :]), ALU.subtract).then_inc(logits_less_max, 1)
                dve.wait_ge(gates_exp, k + 1)
                step(dve.tensor_reduce(gsum[:, :], gt[1][:, :, :], AX_X, ALU.add))
                step(dve.reciprocal(gsum[:, :], gsum[:, :]))
                step(dve.tensor_tensor(gt[2][:, :, :], gt[1][:, :, :], by_tile(gsum[:, :]), ALU.mult))
                step(dve.tensor_reduce(gmax[:, :], gt[2][:, :, :], AX_X, ALU.max))
                dve.tensor_scalar(half_score[:, :], gmax[:, :], 0.5, None, ALU.mult)
                step(dve.tensor_tensor(gt[3][:, :, :], gt[2][:, :, :], by_tile(gmax[:, :]), ALU.is_ge))
                step(dve.tensor_tensor(gt[2][:, :, :], gt[3][:, :, :], rank_weight[:, :].unsqueeze(1).broadcast_to([P, NT, E]), ALU.mult))
                step(dve.tensor_reduce(gsum[:, :], gt[2][:, :, :], AX_X, ALU.max))
                dve.tensor_tensor(onehot[:, :, :], gt[2][:, :, :], by_tile(gsum[:, :]), ALU.is_equal).then_inc(onehot_ready, 1)
                Z = NT // 2
                dve.wait_ge(counts_done, k + 1)
                earlier = PB[7][:, 0:NT * E].rearrange("p (t e) -> p t e", e=E)
                counts = PB[7][:, 128:128 + NT * E].rearrange("p (t e) -> p t e", e=E)
                step(dve.tensor_copy(cum[0][:, Z:Z + NT, :], counts))
                a = 0
                shift = 1
                while shift < NT:
                    step(dve.tensor_tensor(cum[1 - a][:, Z:Z + NT, :], cum[a][:, Z:Z + NT, :], cum[a][:, Z - shift:Z - shift + NT, :], ALU.add))
                    a = 1 - a
                    shift *= 2
                step(dve.tensor_tensor(starts_gt[:, :, :], tile_starts[:, :, :], cum[a][:, Z + NT - 1, :].unsqueeze(2).broadcast_to([P, E, NT]), ALU.is_lt))
                step(dve.tensor_reduce(etiles[:, :], starts_gt[:, :, :], AX_X, ALU.add))
                step(dve.tensor_tensor_scan(etiles_end[:, :], ident_ones, etiles[:, :], 0.0, ALU.mult, ALU.add))
                step(dve.tensor_tensor(ebase[:, :], etiles_end[:, :], etiles[:, :], ALU.subtract))
                step(dve.tensor_scalar(ebase[:, :], ebase[:, :], float(P), None, ALU.mult))
                step(dve.tensor_tensor(gt[0][:, :, :], earlier, cum[a][:, Z - 1:Z - 1 + NT, :], ALU.add))
                step(dve.tensor_tensor(gt[1][:, :, :], gt[0][:, :, :], ebase[:, :].unsqueeze(1).broadcast_to([P, NT, E]), ALU.add))
                step(dve.tensor_tensor(gt[2][:, :, :], gt[1][:, :, :], onehot[:, :, :], ALU.mult))
                step(dve.tensor_reduce(slot_f[:, :], gt[2][:, :, :], AX_X, ALU.add))
                dve.tensor_copy(slot[:, :], slot_f[:, :]).then_inc(slots_ready, 1)
                step(dve.tensor_tensor(tile_ge[:, :, :], slot_tile_no[:, :, :], etiles_end[:, :].unsqueeze(1).broadcast_to([P, ST, E]), ALU.is_ge))
                step(dve.tensor_reduce(tile_expert_f[:, :], tile_ge[:, :, :], AX_X, ALU.add))
                dve.tensor_scalar(tile_expert[:, 1:ST + 1], tile_expert_f[:, :], float(E - 1), None, ALU.min).then_inc(experts_ready, 1)
                dve.wait_ge(experts_ready, k + 1)

            def attention():
                def rest(item):
                    b, z, c = item // 4, item // 2 % 2, item % 2
                    dve.wait_ge(part0_ready, item + 1)
                    if item >= 2:
                        dve.wait_ge(parts_ready, item - 1)
                    dve.tensor_tensor(qk_r[item % 2], qk_f[item % 2], qk_split[z][:, 0, 512 * c:512 * (c + 1)], ALU.subtract).then_inc(rest_ready, 1)

                def middle_part(item):
                    b, z, c = item // 4, item // 2 % 2, item % 2
                    dve.wait_ge(rest_ready, item + 1)
                    dve.tensor_copy(qk_split[z][:, 1, 512 * c:512 * (c + 1)], qk_r[item % 2]).then_inc(part1_ready, 1)

                def last_part(item):
                    b, z, c = item // 4, item // 2 % 2, item % 2
                    dve.wait_ge(part1_ready, item + 1)
                    dve.tensor_tensor(qk_split[z][:, 2, 512 * c:512 * (c + 1)], qk_r[item % 2], qk_split[z][:, 1, 512 * c:512 * (c + 1)], ALU.subtract).then_inc(parts_ready, 1)
                def keep_v():
                    for c in range(4):
                        b = c // 2
                        dve.wait_ge(v_done, c + 1)
                        dve.tensor_tensor(V[:, b * HG:(b + 1) * HG, 4 * (c % 2):4 * (c % 2) + 4, :].rearrange("p g i f -> p i g f"),
                                          PB[c].rearrange("p (i g f) -> p i g f", i=4, g=HG),
                                          b_v[:, :].rearrange("p (g f) -> p g f", g=HG).unsqueeze(1).broadcast_to([P, 4, HG, HG * HD]), ALU.add).then_inc(v_kept, 1)
                for b in range(BATCH):
                    rest(4 * b)
                    for item in range(4 * b, 4 * b + 4):
                        middle_part(item)
                        if item < 4 * b + 3:
                            rest(item + 1)
                        last_part(item)
                    if b == 0:
                        keep_v()


                def maxima(half, u):
                    dve.wait_ge(turn_used, u + 1)
                    dve.tensor_tensor_scan(running_max[half][:, :], restart[:, :], block_max[:, 2 * half:2 * half + 2, :].rearrange("p h b -> p (h b)"),
                                           -LARGE, ALU.min, ALU.max).then_inc(maxima_found, 1)

                def use_turn(u, g, what):
                    bank = turn_bank[parity[0]]
                    parity[0] = (parity[0] + 1) % TB
                    dve.wait_ge(turn_done, u + 1)
                    if what[0] == "out":
                        half = what[1]
                        got = bank.rearrange("p (i h f) -> p i h f", i=4, h=HG)
                        dve.reciprocal(inv_sum[half][:, :, :], got[:, :, :, HD]).then_inc(sums_inverted, 1)
                        dve.wait_ge(sums_inverted, (g.n - 1) * 2 + (half + 1))
                        n = g.n - 1
                        dve.tensor_tensor(attn.rearrange("p (b i f) -> p b i f", b=BATCH, i=KB)[:, bass.ds(n // HG, 1), 4 * half:4 * half + 4, bass.ds(n % HG * (HG * HD), HG * HD)]
                                          .rearrange("p b i (h d) -> p (b i) h d", h=HG), got[:, :, :, 0:HD],
                                          inv_sum[half][:, :, :].unsqueeze(3).broadcast_to([P, 4, HG, HD]), ALU.mult).then_inc(turn_used, 1)
                    elif what[0] == "rows":
                        h, chunk = what[1:]
                        dve.tensor_reduce(block_max[:, h, 4 * chunk:4 * chunk + 4], bank.rearrange("p (j k) -> p j k", k=P), AX_X, ALU.max).then_inc(turn_used, 1)
                        if h % 2 == 1 and chunk == RC - 1:
                            maxima(h // 2, u)
                    else:
                        half = what[1]
                        if g is not before:
                            dve.wait_ge(max_sent[half], (g.n + 1 - half) * 16)
                        dve.tensor_copy(max_rows[half][:, :], bank.bitcast(BF16)[0:PARTS * 2 * KB, 0:P]).then_inc(turn_used, 1)

                parity = [0]
                before = Group(-1, 2, -1)
                for u, what in enumerate(PRO_TURNS):
                    use_turn(u, before, what)

                def steps(g, first, last):
                    u = 0
                    for place in range(3 * CH):
                        for what in turns_at(place, first, last):
                            use_turn((len(PRO_TURNS) if first else turns_before(g.n)) + u, g, what)
                            u += 1
                group_pipeline(dve, steps)
                for half in range(2):
                    use_turn(turns_before(NG - 1) + 3 + half, Group(NG, 0, 0), ("out", half))
                dve.wait_ge(bias_added, 1)
                for c in range(4):
                    dve.wait_ge(proj_done, c + 1)
                    bank = (6, 7, 0, 1)[c]
                    dve.tensor_tensor(X[:, 4 * c:4 * c + 4, :], X[:, 4 * c:4 * c + 4, :], PB[bank].rearrange("p (t d) -> p t d", t=4), ALU.add).then_inc(attended, 1)
                dve.wait_ge(attended, 4)

            def ffn(k):
                B = k * ST
                route(k)
                if k == 0:
                    dve.wait_ge(w1_loaded, 16)

                def stage(q, m, first, e):
                    s, par = q * 4 + m, m % 2
                    if first is None or first >= 2:
                        dve.wait_ge(up_done, s + (B - 1))
                    dve.tensor_copy(W1S[par][:, :], W1[:, bass.ds(e * HID, HID)]).then_inc(w1_staged, 1)

                def bias(q, m, first, e):
                    s, par = q * 4 + m, m % 2
                    dve.wait_ge(up_done, s + (B + 1))
                    if first is None or first >= 2:
                        dve.wait_ge(gelu_done, s + (B - 1))
                    dve.tensor_tensor(HB[par][:, :].rearrange("p (c q) -> p c q", c=HC), PB[2 + par][:, :].rearrange("p (c q) -> p c q", c=HC),
                                      b1_cols[:, bass.ds(e * HC, HC)].unsqueeze(2).broadcast_to([P, HC, P]), ALU.add).then_inc(up_biased, 1)

                def finish(q, m, first, e):
                    s, par = q * 4 + m, m % 2
                    dve.wait_ge(down_done, s + (B + 1))
                    if first is None or first >= 2:
                        dve.wait_ge(y_sent[par], sent(k, q, m))
                    dve.tensor_tensor(YB[par][:, :], PB[4 + par][:, 0:D], b2_all[:, bass.ds(e * D, D)], ALU.add).then_inc(y_ready, 1)

                def steps(q, m, first, last, experts):
                    if last != ST - 1:
                        stage(*after(q, m, 1), None if first is None else first + 1, experts[m + 2])
                    bias(q, m, first, experts[m + 1])
                    if first != 0:
                        finish(*after(q, m, -1), None if first is None else first - 1, experts[m])
                    if last == ST - 1:
                        finish(q, m, None, experts[m + 1])
                stage(0, 0, 0, experts_of(dve, dve_experts)(0)[1])
                tile_pipeline(dve, steps, experts_of(dve, dve_experts))
                dve.wait_ge(y_back, 16 * (k + 1))
                for t in range(NT):
                    ins = dve.scalar_tensor_tensor(out=X[:, t, :], in0=YT[:, t, :], scalar=half_score[:, t:t + 1], in1=X[:, t, :], op0=ALU.mult, op1=ALU.add)
                ins.then_inc(result_ready, 1)
                dve.wait_ge(result_ready, k + 1)

            dve.memset(tile_expert[:, 0:1], 0)
            dve.memset(tile_expert[:, ST + 1:ST + 3], 0)
            ones_e = sb("ones_e", [P, E])
            ident_ones = ones_e[:, :]
            step(dve.memset(ones_e[:, :], 1.0))
            dve.wait_ge(small_loaded, 144)
            step(dve.tensor_tensor(wg_sq[:, :], wg_sb[:, :], wg_sb[:, :], ALU.mult))
            step(dve.tensor_reduce(wg_norm[:, 2:3], wg_sq[:, :], AX_X, ALU.add))
            dve.tensor_scalar(wg_norm[:, 0:1], wg_norm[:, 2:3], NORM_EPS * NORM_EPS, None, ALU.max).then_inc(norm_var, 1)
            dve.wait_ge(norm_std, 1)
            dve.wait_ge(norm_var, 1)
            refine_rsqrt(wg_norm[:, 3:4], wg_norm[:, 0:1], wg_norm[:, 1:2], wg_norm[:, 4:5], wg_norm[:, 5:6])
            dve.tensor_scalar(wg_unit[:, :], wg_sb[:, :], wg_norm[:, 3:4], None, ALU.mult).then_inc(wgu_t_done, 1)
            dve.wait_ge(gate_w_done, 1)
            dve.tensor_copy(wg_unit_t[:, :], PB[6][0:G, 0:E]).then_inc(wgu_t_done, 1)
            dve.wait_ge(gate_w_done, 2)
            dve.tensor_copy(gate_w[:, :], PB[7][:, 0:E]).then_inc(wgu_t_done, 1)
            dve.wait_ge(b1_t_done, 1)
            dve.tensor_copy(b1_cols[:, :], PB[5][:, 0:E * HC])
            dve.wait_ge(attn_w_done, 1)
            dve.tensor_copy(w_attn_t[:, :], PB[4][:, 0:3 * D])
            dve.tensor_copy(b_attn_cols[:, :], PB[5][:, 64:67]).then_inc(attn_w_kept, 1)
            dve.tensor_copy(w_proj_t[:, :], PB[4][:, 3 * D:4 * D]).then_inc(attn_w_kept, 1)
            norm(0, 2)
            ffn(0)
            norm(1, 3)
            attention()
            norm(2, 4)
            ffn(1)


_INS = ['L0_attn_hidden_states', 'L0_attn_w_attn', 'L0_attn_b_attn', 'L0_attn_w_proj', 'L0_attn_b_proj', 'L0_ffn_wg_red',
        'L0_ffn_wg', 'L0_ffn_w1', 'L0_ffn_b1', 'L0_ffn_w2', 'L0_ffn_b2']


_OUTS = [((2, 1024, 128), 'float32')]


def kernel(**inputs):
    import numpy as _np
    import concourse.bacc as _bacc
    from concourse import mybir as _mybir
    from concourse.bass_utils import run_bass_kernel_spmd as _run

    nc = _bacc.Bacc("TRN2", target_bir_lowering=False, num_devices=1)
    arrays, args = {}, []
    for name in _INS:
        a = _np.ascontiguousarray(inputs[name])
        arrays[f"in_{name}_dram"] = a
        args.append(nc.dram_tensor(f"in_{name}_dram", a.shape, _mybir.dt.from_np(a.dtype), kind="ExternalInput").ap())
    for i, (shape, dtype) in enumerate(_OUTS):
        dt = _mybir.dt.from_np(_np.dtype(dtype))
        args.append(nc.dram_tensor(f"out_{i}_dram", shape, dt, kind="ExternalOutput").ap())
    macaron_kernel(nc, *args)
    r = _run(nc, [arrays], core_ids=[0])
    return r.results[0]["out_0_dram"]
```

```python
from contextlib import ExitStack

import concourse.bass as bass
from concourse import mybir

F32 = mybir.dt.float32
BF16 = mybir.dt.bfloat16
I32 = mybir.dt.int32
ALU = mybir.AluOpType
ACT = mybir.ActivationFunctionType
AX_X = mybir.AxisListType.X

P = 128




def macaron_kernel(nc, x, w_attn, b_attn, w_proj, b_proj, wg_red, wg, w1, b1, w2, b2, out):
    BATCH, SEQ, D = x.shape
    TOK = BATCH * SEQ
    NT = TOK // P
    E, G = wg.shape
    HID = w1.shape[2]
    HC = HID // P
    ST = NT + E - 1
    PART_ROW = D + 4
    ROW, NUMBER, STREAM, HALF_GATE = 2 * PART_ROW, D, PART_ROW, PART_ROW + D
    LN_EPS, NORM_EPS = 1e-5, 1e-4
    H, HD = 16, D // 16
    HG = 4
    NG = BATCH * H // HG
    KB = SEQ // P
    PARTS = 3
    TERMS = PARTS * PARTS * HD
    SCALE = float(HD) ** -0.5
    MASKED = -1.0e30
    LARGE = 3.4e38
    assert KB == 8 and NG == 8 and HD == 8
    assert D == P and HC * P == HID and ST % 8 == 7

    x_rows = x.rearrange("b (t p) d -> b p t d", p=P)
    routed = [nc.dram_tensor(f"routed{k}", (ST * P, ROW), F32, kind="Internal").ap() for k in range(2)]
    stream = [nc.dram_tensor("stream0", (TOK, D), F32, kind="Internal").ap(), out.rearrange("b s d -> (b s) d")]

    q_parts = nc.dram_tensor("q_parts", (NG * HG, PARTS * HD, SEQ), BF16, kind="Internal").ap()
    k_parts = nc.dram_tensor("k_parts", (NG * HG, (2 * PARTS - 1) * HD, SEQ), BF16, kind="Internal").ap()

    ROW_CHUNKS = [[(7, 0, 512, 0)], [(7, 512, 512, 0)], [(6, 0, 512, 0)], [(6, 512, 384, 0), (0, 0, 128, 384)],
                  [(5, 0, 512, 0)], [(5, 512, 256, 0), (1, 0, 256, 256)], [(4, 0, 512, 0)],
                  [(4, 512, 128, 0), (2, 0, 384, 128)], [(3, 0, 512, 0)]]
    ROW_MAXIMA = {7: (0, 8), 6: (8, 15), 0: (15, 16), 5: (16, 22), 1: (22, 24), 4: (24, 29), 2: (29, 32), 3: (32, 36)}
    RC = len(ROW_CHUNKS)

    def key_chunk(t):
        if t >= 16:
            return [(2 * (t - 16) + e, 4, 512 * e - 512) for e in range(2)]
        j = t // 4
        return [(t % 4, j, -128 * j)] + ([(t % 4, 8 - j, 0)] if j else [])
    CH = 18
    PIECES = [(0, 0, 256), (0, 256, 256), (0, 512, 256), (0, 768, 256),
              (1, 128, 384), (1, 512, 256), (1, 768, 256), (7, 896, 128),
              (2, 256, 256), (2, 512, 256), (2, 768, 256), (6, 768, 256),
              (3, 384, 128), (3, 512, 256), (3, 768, 256), (5, 640, 384),
              (4, 512, 256), (4, 768, 256)]
    LAG = 5
    HALF_DONE = (13, 18)
    PROBS = 9

    def last_piece(t):
        return CH - 1 if t >= 16 else 4 * (t // 4) + 3

    ROW_TURNS = [("rows", k // RC, k % RC) for k in range(HG * RC)]
    OUT_AT, MAXIMA_AT = (4, 20), (32, 1)
    MAXIMA1_AT_FIRST = 4
    ROWS_UNTIL = 46
    BATCH0_AT = {("turned", 0): 8, ("turned", 1): 11, ("projected", 0): 14, ("projected", 1): 17}

    def turns_at(place, first=False, last=False):
        out = [("maxima", 1)] if place == (MAXIMA1_AT_FIRST if first else MAXIMA_AT[1]) else []
        out += [("out", h) for h in range(2) if OUT_AT[h] == place and not first]
        if last:
            out += [turn for turn, at in BATCH0_AT.items() if at == place]
        else:
            out += [r for k, r in enumerate(ROW_TURNS) if k * ROWS_UNTIL // len(ROW_TURNS) == place]
            out += [("maxima", 0)] if place == MAXIMA_AT[0] else []
        return out
    MIDDLE_TURNS = [turn for place in range(3 * CH) for turn in turns_at(place)]
    LAST_TURNS = [turn for place in range(3 * CH) for turn in turns_at(place, last=True)]
    PRO_TURNS = ROW_TURNS[:26] + [("maxima", 0)] + ROW_TURNS[26:]
    FIRST_TURNS = [turn for place in range(3 * CH) for turn in turns_at(place, first=True)]
    GT = len(MIDDLE_TURNS)
    TB = 3

    def turns_before(g):
        return g * GT + (len(PRO_TURNS) + len(FIRST_TURNS) - GT)

    class Group:
        def __init__(self, n, slot, turn):
            self.n, self.slot, self.turn = n, slot, turn

        def plus(self, d):
            return Group(self.n + d, (self.slot + d) % 3, self.turn + (self.slot + d) // 3)

    with ExitStack() as ctx:
        def sb(name, shape, dt=F32):
            return ctx.enter_context(nc.sbuf_tensor(name, shape, dt))

        def sem(name):
            return ctx.enter_context(nc.semaphore(name))

        ident = sb("ident", [P, P])
        ones_bf = sb("ones_bf", [P, P], BF16)
        before_bf = sb("before_bf", [P, P], BF16)
        rank_weight = sb("rank_weight", [P, E])
        tile_starts = sb("tile_starts", [P, E, NT])
        slot_tile_no = sb("slot_tile_no", [P, ST, E])
        blank = sb("blank", [P, ROW])

        W1 = sb("W1", [P, E * HID])
        W2 = sb("W2", [P, E * HC * D])
        b1_rows = sb("b1_rows", [E * HC, P])
        b1_cols = sb("b1_cols", [P, E * HC])
        b2_all = sb("b2_all", [P, E * D])
        wg_red_sb = sb("wg_red_sb", [G, D])
        wg_sb = sb("wg_sb", [E, G])
        wg_sq = sb("wg_sq", [E, G])
        wg_norm = sb("wg_norm", [E, 6])
        wg_unit = sb("wg_unit", [E, G])
        wg_unit_t = sb("wg_unit_t", [G, E])
        gate_w = sb("gate_w", [P, E])

        X = sb("X", [P, NT, D])
        XR = sb("XR", [P, NT, ROW])
        XT = sb("XT", [P, TOK])
        YT = sb("YT", [P, NT, D])
        w_attn_sb = sb("w_attn_sb", [P, 3, D])
        w_proj_sb = sb("w_proj_sb", [P, D])
        w_attn_t = sb("w_attn_t", [P, 3 * D])
        w_proj_t = sb("w_proj_t", [P, D])
        b_attn_rows = sb("b_attn_rows", [3, D])
        b_attn_cols = sb("b_attn_cols", [P, 3])
        b_v = sb("b_v", [P, D])
        b_p = sb("b_p", [P, D])
        ident_bf = sb("ident_bf", [P, P], BF16)
        row_mask = sb("row_mask", [P, P], BF16)
        key_mask = sb("key_mask", [P, P], BF16)
        QK = sb("QK", [P, 3, 2, HG, SEQ], BF16)
        probs = sb("probs", [P, PROBS, SEQ])
        V = sb("V", [P, NG, KB, HG * HD])
        VS = sb("VS", [P, 3, KB, HG, 32])
        block_max = sb("block_max", [P, HG, 4 * RC])
        zeros = sb("zeros", [P, 2, KB])
        restart = sb("restart", [P, 2 * 4 * RC])
        running_max = [sb(f"running_max{i}", [P, 2 * 4 * RC]) for i in range(2)]
        row_max = [sb(f"row_max{i}", [P, 2, KB]) for i in range(2)]
        max_rest = [sb(f"max_rest{i}", [P, 2, KB]) for i in range(2)]
        max_parts_all = [sb(f"max_parts{i}", [P, P], BF16) for i in range(2)]
        max_parts = [a[:, 0:PARTS * 2 * KB].rearrange("p (a h i) -> p a h i", a=PARTS, h=2) for a in max_parts_all]
        max_rows = [sb(f"max_rows{i}", [PARTS * 2 * KB, P], BF16) for i in range(2)]
        inv_sum = [sb(f"inv_sum{i}", [P, 4, HG]) for i in range(2)]
        stats = sb("stats", [P, NT, 6])
        mean_var = sb("mean_var", [P, NT, 2])
        var_eps = sb("var_eps", [P, NT])
        std = sb("std", [P, NT])
        rstd = sb("rstd", [P, NT])
        newton_a = sb("newton_a", [P, NT])
        newton_b = sb("newton_b", [P, NT])

        gt = [sb(f"gt{i}", [P, NT, E]) for i in range(4)]
        gmax = sb("gmax", [P, NT])
        gsum = sb("gsum", [P, NT])
        onehot = sb("onehot", [P, E, NT], BF16)
        cum = sb("cum", [P, E, NT])
        go_on = sb("go_on", [P, E, NT])
        etiles = sb("etiles", [P, E])
        etiles_end = sb("etiles_end", [P, E])
        etiles_start = sb("etiles_start", [P, E])
        tile_used = sb("tile_used", [P, E, NT])
        slot_f = sb("slot_f", [P, NT])
        slot = sb("slot", [P, NT], I32)
        ones_e = sb("ones_e", [P, E])
        tile_ge = sb("tile_ge", [P, ST, E])
        tile_expert_f = sb("tile_expert_f", [P, ST])
        tile_expert = sb("tile_expert", [P, ST + 3], I32)

        shared = probs[:, :, :].rearrange("p c q -> p (c q)")
        taken = [0]

        def of_shared(width):
            taken[0] += width
            return shared[:, taken[0] - width:taken[0]]
        XS = [of_shared(PART_ROW) for i in range(4)]
        XG = [of_shared(PART_ROW) for i in range(4)]
        XST = [of_shared(P) for i in range(2)]
        W1S = [of_shared(HID) for i in range(2)]
        HB = [of_shared(HID) for i in range(2)]
        HT = [of_shared(HID) for i in range(2)]
        YB = [of_shared(D) for i in range(2)]
        token_nos = sb("token_nos", [P, ST], I32)
        token_no = [sb(f"token_no{i}", [P, 1], I32) for i in range(2)]

        qk_f = [YT[:, 8 * i:8 * i + 4, :].rearrange("p a d -> p (a d)") for i in range(2)]
        qk_r = [YT[:, 8 * i + 4:8 * i + 8, :].rearrange("p a d -> p (a d)") for i in range(2)]
        split = probs[:, PROBS - PARTS:PROBS, :].rearrange("p c t -> p (c t)").bitcast(BF16)
        qk_split = [split[:, PARTS * SEQ * z:PARTS * SEQ * (z + 1)].rearrange("p (a t) -> p a t", a=PARTS) for z in range(2)]
        attn = YT[:, :, :].rearrange("p t d -> p (t d)")
        out_t = XT[:, 0:SEQ]
        attn_t = [XT[:, 512 * ((c + 2) % 4):512 * ((c + 2) % 4 + 1)] for c in range(4)]

        PS = ctx.enter_context(nc.psum_tensor("PS", [P, 8 * 512], F32))
        PB = [PS[:, 512 * i:512 * (i + 1)] for i in range(8)]
        turn_bank, key_bank = PB[0:TB], PB[3:6]
        out_acc = PS[:, 3072:4096]

        x_loaded = [sem(f"x_loaded{b}") for b in range(BATCH)]
        small_loaded = sem("small_loaded")
        w1_loaded, w2_loaded = sem("w1_loaded"), sem("w2_loaded")
        consts_made = sem("consts_made")
        blank_ready = sem("blank_ready")
        pool_step = sem("pool_step")
        dve_step = sem("dve_step")
        blanked = [sem(f"blanked{k}") for k in range(2)]
        wgu_t_done, gate_w_done, b1_t_done = sem("wgu_t_done"), sem("gate_w_done"), sem("b1_t_done")
        norm_var, norm_std = sem("norm_var"), sem("norm_std")
        gate_var, gate_std = sem("gate_var"), sem("gate_std")
        norm_rows = sem("norm_rows")
        rows_turned, turned_kept = sem("rows_turned"), sem("turned_kept")
        logits_done, logits_less_max, gates_exp = sem("logits_done"), sem("logits_less_max"), sem("gates_exp")
        onehot_ready, counts_done = sem("onehot_ready"), sem("counts_done")
        slots_ready, experts_ready = sem("slots_ready"), sem("experts_ready")
        rows_routed = sem("rows_routed")
        xs_loaded = [sem(f"xs_loaded{i}") for i in range(4)]
        xg_loaded = [sem(f"xg_loaded{i}") for i in range(4)]
        xs_turned, xst_kept = sem("xs_turned"), sem("xst_kept")
        w1_staged = sem("w1_staged")
        up_done, up_biased, gelu_done = sem("up_done"), sem("up_biased"), sem("gelu_done")
        down_done, y_ready = sem("down_done"), sem("y_ready")
        token_no_kept, token_no_at_pool = sem("token_no_kept"), sem("token_no_at_pool")
        y_sent = [sem(f"y_sent{i}") for i in range(2)]
        x_back = [sem(f"x_back{c}") for c in range(4)]
        x_copied, y_biased = sem("x_copied"), sem("y_biased")
        attn_w_done, attn_w_kept = sem("attn_w_done"), sem("attn_w_kept")
        qk_done, qk_kept, part0_ready, rest_ready, part1_ready = (sem(n) for n in ("qk_done", "qk_kept", "part0_ready", "rest_ready", "part1_ready"))
        parts_ready, parts_sent = sem("parts_ready"), [sem(f"parts_sent{z}") for z in range(2)]
        v_done, v_kept, v_staged = sem("v_done"), sem("v_kept"), sem("v_staged")
        qk_loaded = [sem(f"qk_loaded{i}") for i in range(3)]
        ones_set = sem("ones_set")
        turn_done, turn_used = sem("turn_done"), sem("turn_used")
        maxima_found, max_step, max_parts_ready = sem("maxima_found"), sem("max_step"), sem("max_parts_ready")
        max_sent = [sem(f"max_sent{h}") for h in range(2)]
        scores_done, probs_ready, pieces_done, out_kept, sums_inverted = (sem(n) for n in ("scores_done", "probs_ready", "pieces_done", "out_kept", "sums_inverted"))
        attn_turned, attn_kept, proj_done = sem("attn_turned"), sem("attn_kept"), sem("proj_done")
        bias_added, attended = sem("bias_added"), sem("attended")

        PROJ_BANKS = {2: 6, 3: 7}

        def last_turn(what):
            return turns_before(NG - 1) + LAST_TURNS.index(what) + 1

        def of_item(item):
            return item // 4, 1 - item // 2 % 2, item % 2

        def half_tiles(h):
            return slice(NT // 2 * h, NT // 2 * (h + 1))

        def loaded(k, q, m):
            return q * 16 + 16 * (k * ((ST - 1 - m) // 4 + 1) + 1)

        def sent(k, q, m):
            return q * 32 + 16 * (k * ((ST + 1 - m % 2) // 2) + m // 2)

        def after(q, m, d):
            return q + (m + d) // 4, (m + d) % 4

        def experts_of(engine, registers):
            def load(q, count):
                engine.load(registers[0:count], tile_expert[0:1, bass.ds(q * 4, count)])
                return [engine.snap(r, min_val=0, max_val=E - 1) for r in registers[0:count]]
            return load

        def tile_pipeline(engine, steps, begin=lambda q, count: [None] * count):
            at_q = begin(0, 6)
            for m in range(4):
                steps(0, m, m, None, at_q)
            with engine.Fori(0, (ST - 7) // 8) as i:
                at_q = begin(i * 2 + 1, 10)
                for half in range(2):
                    for m in range(4):
                        steps(i * 2 + (1 + half), m, None, None, at_q[4 * half:])
            at_q = begin((ST - 3) // 4, 6)
            for m in range(3):
                steps((ST - 3) // 4, m, None, ST - 3 + m, at_q)

        def max_turn(g, half):
            if isinstance(g.n, int) and g.n == 0:
                return len(PRO_TURNS) + FIRST_TURNS.index(("maxima", 1)) + 1 if half else PRO_TURNS.index(("maxima", 0)) + 1
            if isinstance(g.n, int) and g.n == NG - 1 and half:
                return turns_before(g.n) + 1
            return turns_before(g.n - (1 - half)) + (MIDDLE_TURNS.index(("maxima", half)) + 1)

        def out_turn(g, half):
            return turns_before(g.n + 1) + (MIDDLE_TURNS.index(("out", half)) + 1)

        def group_pipeline(engine, steps):
            steps(Group(0, 0, 0), True, False)
            with engine.Fori(0, (NG - 2) // 3) as i:
                for j in range(3):
                    steps(Group(i * 3 + (1 + j), (1 + j) % 3, i + (1 + j) // 3), False, False)
            steps(Group(NG - 1, (NG - 1) % 3, (NG - 1) // 3), False, True)

        block = ctx.enter_context(nc.Block())

        @block.sync
        def _(sp):
            for b in range(BATCH):
                sp.dma_start(X[:, b * NT // BATCH:(b + 1) * NT // BATCH, :], x_rows[b]).then_inc(x_loaded[b], 16)
            sp.dma_start(wg_red_sb[:, :], wg_red).then_inc(small_loaded, 16)
            sp.dma_start(wg_sb[:, :], wg).then_inc(small_loaded, 16)
            sp.dma_start(b1_rows[:, :], b1.rearrange("e (c p) -> (e c) p", p=P)).then_inc(small_loaded, 16)
            sp.dma_start(b2_all[:, :], b2.rearrange("(o e) d -> o (e d)", o=1).broadcast_to([P, E * D])).then_inc(small_loaded, 16)
            sp.dma_start(w_attn_sb[:, :, :], w_attn.rearrange("(a p) d -> p a d", p=P)).then_inc(small_loaded, 16)
            sp.dma_start(w_proj_sb[:, :], w_proj).then_inc(small_loaded, 16)
            sp.dma_start(b_attn_rows[:, :], b_attn.rearrange("(a d) -> a d", a=3)).then_inc(small_loaded, 16)
            sp.dma_start(b_v[:, :], b_attn[2 * D:3 * D].rearrange("(o d) -> o d", o=1).broadcast_to([P, D])).then_inc(small_loaded, 16)
            sp.dma_start(b_p[:, :], b_proj.rearrange("(o d) -> o d", o=1).broadcast_to([P, D])).then_inc(small_loaded, 16)
            sp.dma_start(W1[:, :].rearrange("p (e h) -> p e h", e=E), w1.rearrange("e p h -> p e h")).then_inc(w1_loaded, 16)
            sp.dma_start(W2[:, :].rearrange("p (e c d) -> p e c d", e=E, c=HC), w2.rearrange("e (c p) d -> p e c d", p=P)).then_inc(w2_loaded, 16)
            sp.wait_ge(blank_ready, 1)
            for k in range(2):
                sp.dma_start(routed[k].rearrange("(s p) r -> p s r", p=P), blank[:, :].unsqueeze(1).broadcast_to([P, ST, ROW])).then_inc(blanked[k], 16)

            def ffn(k):
                B = k * ST

                def load(q, m, first, last, _):
                    s = q * 4 + m
                    if first is None:
                        sp.wait_ge(xs_turned, s + (B - 3))
                        sp.wait_ge(token_no_kept, s + (B - 3))
                    sp.dma_start(XS[m][:, :], routed[k][bass.ds(s * P, P), 0:PART_ROW]).then_inc(xs_loaded[m], 16)
                    for back in (2, 1, 0) if last == ST - 1 else (2,):
                        if first is None or first >= back:
                            load_stream(*after(q, m, -back), first is None)

                def load_stream(q, m, refill):
                    s = q * 4 + m
                    if refill:
                        sp.wait_ge(w1_staged, s + B)
                    sp.dma_start(XG[m][:, :], routed[k][bass.ds(s * P, P), PART_ROW:ROW]).then_inc(xg_loaded[m], 16)
                sp.wait_ge(rows_routed, 16 * NT * (k + 1))
                tile_pipeline(sp, load)
                for par in range(2):
                    sp.wait_ge(y_sent[par], 16 * (k + 1) * ((ST + 1 - par) // 2))
                if k == 0:
                    for c in range(4):
                        part = TOK // 4
                        sp.dma_start(X[:, NT // 4 * c:NT // 4 * (c + 1), :], stream[k][part * c:part * (c + 1), :].rearrange("(t p) d -> p t d", p=P)).then_inc(x_back[c], 16)

            def attention():
                def send_parts(b):
                    for z, parts in ((1, k_parts), (0, q_parts)):
                        for block_no in range(PARTS if z == 0 else 2 * PARTS - 1):
                            if block_no < PARTS:
                                sp.wait_ge(parts_ready, 4 * b + 4 - 2 * z)
                            sp.dma_start(parts[b * H:(b + 1) * H, block_no * HD:(block_no + 1) * HD, :],
                                         qk_split[z][:, block_no % PARTS, :]).then_inc(parts_sent[z], 16)

                def wait_sent(b, z):
                    sp.wait_ge(parts_sent[z], 16 * (b + 1) * (PARTS if z == 0 else 2 * PARTS - 1))

                def load(g, z):
                    for r in range(PARTS):
                        parts = q_parts[bass.ds(g.n * HG, HG), :, :] if z == 0 else k_parts[bass.ds(g.n * HG, HG), 8 * r:8 * r + 24, :]
                        sp.dma_start(QK[24 * r:24 * r + 24, g.slot, z, :, :], parts.rearrange("h r t -> r h t")).then_inc(qk_loaded[g.slot], 16)

                def send_max(g, half):
                    sp.wait_ge(turn_used, max_turn(g, half))
                    sp.dma_start(QK[TERMS:TERMS + PARTS, g.slot, 0, 2 * half:2 * half + 2, :], max_rows[half][:, :]).then_inc(max_sent[half], 16)
                send_parts(0)
                sp.wait_ge(ones_set, 3)
                for z in (1, 0):
                    wait_sent(0, z)
                    load(Group(0, 0, 0), z)
                for z in (1, 0):
                    load(Group(1, 1, 0), z)
                send_parts(1)
                for z in (1, 0):
                    wait_sent(1, z)
                for half in range(2):
                    send_max(Group(0, 0, 0), half)
                with sp.Fori(0, (NG - 2) // 3) as i:
                    for j in range(3):
                        g = Group(i * 3 + j, j, i)
                        sp.wait_ge(scores_done, g.n * (2 * CH) + 1)
                        for z in (1, 0):
                            load(g.plus(2), z)
                        for half in range(2):
                            send_max(g.plus(1), half)
                for half in range(2):
                    send_max(Group(NG - 1, (NG - 1) % 3, (NG - 1) // 3), half)
            ffn(0)
            attention()
            ffn(1)

        @block.gpsimd
        def _(pool):
            n = [0]

            def step(ins):
                n[0] += 1
                ins.then_inc(pool_step, 1)
                pool.wait_ge(pool_step, n[0])

            step(pool.memset(XR[:, :, NUMBER:PART_ROW], 0.0))
            step(pool.memset(XR[:, :, HALF_GATE:ROW], 0.0))
            step(pool.iota(XR[:, :, NUMBER:NUMBER + 1].bitcast(I32).rearrange("p s o -> p (s o)"), [[P, NT]], base=0, channel_multiplier=1))
            step(pool.memset(ident[:, :], 0.0))
            pool.affine_select(out=ident[:, :], in_=ident[:, :], compare_op=ALU.not_equal, fill=1.0, base=0, pattern=[[-1, P]], channel_multiplier=1).then_inc(consts_made, 1)
            pool.wait_ge(consts_made, 1)
            step(pool.memset(blank[:, :], 0.0))
            pool.iota(blank[:, NUMBER:NUMBER + 1].bitcast(I32), [[0, 1]], base=TOK, channel_multiplier=0).then_inc(blank_ready, 1)
            pool.wait_ge(blank_ready, 1)
            step(pool.memset(ones_bf[:, :], 1.0))
            step(pool.memset(before_bf[:, :], 0.0))
            step(pool.affine_select(out=before_bf[:, :], in_=before_bf[:, :], compare_op=ALU.is_gt, fill=-1.0, base=0, pattern=[[1, P]], channel_multiplier=-1))
            step(pool.memset(row_mask[:, :], 0.0))
            step(pool.affine_select(out=row_mask[:, :], in_=row_mask[:, :], compare_op=ALU.is_ge, fill=MASKED, base=0, pattern=[[-1, P]], channel_multiplier=1))
            step(pool.memset(key_mask[:, :], 0.0))
            step(pool.affine_select(out=key_mask[:, :], in_=key_mask[:, :], compare_op=ALU.is_ge, fill=MASKED, base=0, pattern=[[1, P]], channel_multiplier=-1))
            step(pool.tensor_copy(ident_bf[:, :], ident[:, :]))
            step(pool.memset(VS[:, :, :, :, :], 0.0))
            for half in range(2):
                step(pool.memset(max_parts_all[half][:, :], 0.0))
            step(pool.memset(VS[:, :, :, :, HD:HD + 1], 1.0))
            step(pool.memset(zeros[:, :, :], 0.0))
            step(pool.memset(restart[:, :], LARGE))
            for a, z in ROW_MAXIMA.values():
                ins = pool.memset(restart[:, :].rearrange("p (h b) -> p h b", h=2)[:, :, a:a + 1], -LARGE)
            step(ins)
            step(pool.iota(rank_weight[:, :], [[-1, E]], base=E, channel_multiplier=0, allow_small_or_imprecise_dtypes=True))
            step(pool.iota(tile_starts[:, :, :], [[0, E], [P, NT]], base=0, channel_multiplier=0, allow_small_or_imprecise_dtypes=True))
            step(pool.iota(slot_tile_no[:, :, :], [[1, ST], [0, E]], base=0, channel_multiplier=0, allow_small_or_imprecise_dtypes=True))
            step(pool.memset(go_on[:, :, :], 1.0))
            pool.memset(go_on[:, :, 0:1], 0.0).then_inc(consts_made, 1)
            pool.wait_ge(consts_made, 2)
            for slot_no in range(3):
                pool.memset(QK[64:96, slot_no, 1, :, :], -1.0).then_inc(ones_set, 1)
                pool.wait_ge(ones_set, slot_no + 1)

            def ffn(k):
                B = k * ST
                pool.wait_ge(slots_ready, k + 1)
                pool.wait_ge(blanked[k], 16)
                pool.wait_ge(x_copied, 4 * (k + 1))
                for t in range(NT):
                    pool.indirect_dma_start(routed[k], bass.IndirectOffsetOnAxis(ap=slot[:, t:t + 1], axis=0),
                                            XR[:, t, :], None).then_inc(rows_routed, 16)

                def send(q, m, first, last, _):
                    s, par = q * 4 + m, m % 2
                    pool.wait_ge(token_no_kept, s + (B + 1))
                    if first is None or first >= 2:
                        pool.wait_ge(y_sent[par], sent(k, q, m))
                    pool.tensor_copy(token_no[par][:, :], token_nos[:, bass.ds(s, 1)]).then_inc(token_no_at_pool, 1)
                    pool.wait_ge(slots_ready, k + 1)
                    pool.wait_ge(token_no_at_pool, s + (B + 1))
                    pool.wait_ge(y_ready, s + (B + 1))
                    pool.indirect_dma_start(stream[k], bass.IndirectOffsetOnAxis(ap=token_no[par][:, 0:1], axis=0),
                                            YB[par][:, :], None, bounds_check=TOK - 1, oob_is_err=False).then_inc(y_sent[par], 16)
                tile_pipeline(pool, send)

            def attention():
                pool.wait_ge(norm_rows, 2 * NT)
                pool.tensor_tensor(X[:, :, :], X[:, :, :], b_p[:, :].unsqueeze(1).broadcast_to([P, NT, D]), ALU.add).then_inc(bias_added, 1)

                def stage(g):
                    pool.tensor_copy(VS[:, g.slot, :, :, 0:HD], V[:, :, :, :].rearrange("p g i f -> p (g i f)")[:, bass.ds(g.n * (KB * HG * HD), KB * HG * HD)]
                                     .rearrange("p (i h d) -> p i h d", i=KB, h=HG)).then_inc(v_staged, 1)

                def split_maxima(g, half):
                    base = g.n * 8 + 4 * half

                    def link(ins, k):
                        ins.then_inc(max_step, 1)
                        pool.wait_ge(max_step, base + k)
                    pool.wait_ge(maxima_found, g.n * 2 + (half + 1))
                    for i, (a, z) in ROW_MAXIMA.items():
                        ins = pool.tensor_tensor(row_max[half][:, :, i:i + 1], running_max[half][:, :].rearrange("p (h b) -> p h b", h=2)[:, :, z - 1:z], zeros[:, :, 0:1], ALU.add)
                    link(ins, 1)
                    link(pool.tensor_tensor(max_parts[half][:, 0], row_max[half][:, :, :], zeros[:, :, :], ALU.add), 2)
                    link(pool.tensor_tensor(max_rest[half][:, :, :], row_max[half][:, :, :], max_parts[half][:, 0], ALU.subtract), 3)
                    link(pool.tensor_tensor(max_parts[half][:, 1], max_rest[half][:, :, :], zeros[:, :, :], ALU.add), 4)
                    pool.tensor_tensor(max_parts[half][:, 2], max_rest[half][:, :, :], max_parts[half][:, 1], ALU.subtract).then_inc(max_parts_ready, 1)
                pool.wait_ge(v_kept, 4)
                stage(Group(0, 0, 0))
                stage(Group(1, 1, 0))
                for half in range(2):
                    split_maxima(Group(0, 0, 0), half)
                with pool.Fori(0, (NG - 2) // 3) as i:
                    for j in range(3):
                        g = Group(i * 3 + j, j, i)
                        pool.wait_ge(v_kept, 4)
                        pool.wait_ge(pieces_done, g.n * CH + 1)
                        stage(g.plus(2))
                        for half in range(2):
                            split_maxima(g.plus(1), half)
                for half in range(2):
                    split_maxima(Group(NG - 1, (NG - 1) % 3, (NG - 1) // 3), half)
            ffn(0)
            attention()
            ffn(1)

        @block.scalar
        def _(act):
            def norm(q, h):
                if q == 0 and h == 1:
                    act.wait_ge(gate_var, 1)
                    act.activation(wg_norm[:, 1:2], wg_norm[:, 0:1], ACT.Sqrt).then_inc(gate_std, 1)
                act.wait_ge(norm_var, 2 * q + h + 1)
                act.activation(std[:, half_tiles(h)], var_eps[:, half_tiles(h)], ACT.Sqrt).then_inc(norm_std, 1)

            def keep_rows(q, first=0, count=2):
                for c in range(first, first + count):
                    act.wait_ge(rows_turned, 4 * q + c + 1)
                    act.activation(XT[:, c * 512:(c + 1) * 512], PB[c][:, :], ACT.Copy).then_inc(turned_kept, 1)

            def ffn(k):
                B = k * ST
                keep_rows(2 * k, 0, 4)
                act.wait_ge(logits_less_max, k + 1)
                act.activation(gt[1][:, :, :], gt[0][:, :, :], ACT.Exp).then_inc(gates_exp, 1)
                for c in range(4):
                    if k == 0:
                        act.wait_ge(x_loaded[c // 2], 16)
                    else:
                        act.wait_ge(attended, max(c - 1, 1))
                    act.activation(XR[:, NT // 4 * c:NT // 4 * (c + 1), STREAM:STREAM + D], X[:, NT // 4 * c:NT // 4 * (c + 1), :], ACT.Copy).then_inc(x_copied, 1)

                def keep_turned(q, m, first):
                    s, par = q * 4 + m, m % 2
                    act.wait_ge(xs_turned, s + (B + 1))
                    if first is None or first >= 2:
                        act.wait_ge(up_done, s + (B - 1))
                    act.activation(XST[par][:, :], PB[par][:, 0:P], ACT.Copy).then_inc(xst_kept, 1)
                    act.activation(token_nos[:, bass.ds(s, 1)], XS[m][:, NUMBER:NUMBER + 1].bitcast(I32), ACT.Copy).then_inc(token_no_kept, 1)

                def gelu(q, m, first):
                    s, par = q * 4 + m, m % 2
                    act.wait_ge(up_biased, s + (B + 1))
                    if first is None or first >= 2:
                        act.wait_ge(down_done, s + (B - 1))
                    act.activation(HT[par][:, :], HB[par][:, :], ACT.Gelu).then_inc(gelu_done, 1)

                def steps(q, m, first, last, experts):
                    if last != ST - 1:
                        keep_turned(*after(q, m, 1), None if first is None else first + 1)
                    gelu(q, m, first)
                keep_turned(0, 0, 0)
                tile_pipeline(act, steps)

            def attention():
                for item in range(4 * BATCH):
                    if item % 4 == 0:
                        keep_rows(1, 2 * (item // 4))
                    b, z, c = of_item(item)
                    act.wait_ge(qk_done, item + 1)
                    if item >= 2:
                        act.wait_ge(rest_ready, item - 1)
                    act.activation(qk_f[item % 2], PB[4 + item % 4], ACT.Identity, bias=b_attn_cols[:, z:z + 1]).then_inc(qk_kept, 1)
                    act.wait_ge(qk_kept, item + 1)
                    if b and c == 0:
                        act.wait_ge(parts_sent[z], 16 * (PARTS if z == 0 else 2 * PARTS - 1))
                    act.activation(qk_split[z][:, 0, 512 * c:512 * (c + 1)], qk_f[item % 2], ACT.Copy).then_inc(part0_ready, 1)


                def keep_out(g, half, final=False):
                    act.wait_ge(pieces_done, g.n * CH + HALF_DONE[half])
                    act.wait_ge(turn_done, last_turn(("out", half)) if final else out_turn(g, half) - GT)
                    act.activation(out_t[:, 512 * half:512 * (half + 1)], out_acc[:, 512 * half:512 * (half + 1)], ACT.Copy).then_inc(out_kept, 1)

                def steps(g, first, last):
                    for t in range(CH):
                        if not first and t == 0:
                            keep_out(g.plus(-1), 0)
                        if not first and t == LAG:
                            keep_out(g.plus(-1), 1)
                        if t >= PROBS:
                            act.wait_ge(pieces_done, g.n * CH + (last_piece(t - PROBS) + 1))
                        elif not first:
                            act.wait_ge(pieces_done, (g.n - 1) * CH + (last_piece(t + PROBS) + 1))
                        for c in range(2):
                            act.wait_ge(scores_done, g.n * (2 * CH) + (2 * t + c + 1))
                            act.activation(probs[:, t % PROBS, 512 * c:512 * (c + 1)], key_bank[(2 * t + c) % 3], ACT.Exp, scale=SCALE).then_inc(probs_ready, 1)
                act.wait_ge(parts_sent[0], 16 * BATCH * PARTS)
                act.wait_ge(parts_sent[1], 16 * BATCH * (2 * PARTS - 1))
                group_pipeline(act, steps)
                keep_out(Group(NG - 1, 0, 0), 0, True)
                norm(2, 0)
                keep_out(Group(NG - 1, 0, 0), 1, True)
                for c in (2, 3):
                    act.wait_ge(attn_turned, c - 1)
                    act.activation(attn_t[c], PB[c], ACT.Copy).then_inc(attn_kept, 1)
                norm(2, 1)
            for h in range(2):
                norm(0, h)
            ffn(0)
            for h in range(2):
                norm(1, h)
            attention()
            ffn(1)

        @block.tensor
        def _(pe):
            pe_experts = [pe.alloc_register(f"pe_expert{j}") for j in range(10)]
            def turn_rows(q, turned=lambda c: None):
                for t in range(NT):
                    pe.wait_ge(norm_rows, NT * q + t + 1)
                    mm = pe.transpose(PB[t // 4][:, (t % 4) * P:(t % 4 + 1) * P], XR[:, t, 0:D], ident[:, :])
                    if t % 4 == 3:
                        mm.then_inc(rows_turned, 1)
                        turned(t // 4)

            def gate_weights():
                pe.wait_ge(wgu_t_done, 1)
                pe.transpose(PB[6][0:G, 0:E], wg_unit[:, :], ident[0:E, 0:E]).then_inc(gate_w_done, 1)
                pe.wait_ge(wgu_t_done, 2)
                pe.matmul(PB[7][:, 0:E], wg_red_sb[:, :], wg_unit_t[:, :], start=True, stop=True).then_inc(gate_w_done, 1)
                pe.wait_ge(wgu_t_done, 3)

            def turn_weights():
                for a in range(3):
                    pe.transpose(PB[4][:, a * P:(a + 1) * P], w_attn_sb[:, a, :], ident[:, :])
                pe.transpose(PB[4][:, 3 * P:4 * P], w_proj_sb[:, :], ident[:, :]).then_inc(attn_w_done, 1)
                pe.transpose(PB[5][:, 64:67], b_attn_rows[:, :], ident[0:3, 0:3])
                pe.transpose(PB[5][:, 0:E * HC], b1_rows[:, :], ident[0:E * HC, 0:E * HC]).then_inc(b1_t_done, 1)

            def ffn(k):
                B = k * ST

                def logits(c):
                    pe.wait_ge(turned_kept, 8 * k + c + 1)
                    for t in range(4 * c, 4 * c + 4):
                        mm = pe.matmul(PB[6][:, t * E:(t + 1) * E], XT[:, t * P:(t + 1) * P], gate_w[:, :], start=True, stop=True)
                    if c == 3:
                        mm.then_inc(logits_done, 1)

                def turned(c):
                    if k == 0 and c == 1:
                        gate_weights()
                    if c >= 1:
                        logits(c - 1)
                    if c == 3:
                        logits(3)
                turn_rows(2 * k, turned)
                if k == 0:
                    turn_weights()
                pe.wait_ge(consts_made, 2)
                pe.wait_ge(onehot_ready, k + 1)
                pe.matmul(PB[7][:, 0:NT * E], before_bf[:, :], onehot[:, :, :].rearrange("p e t -> p (e t)"), start=True, stop=True)
                pe.matmul(PB[7][:, 128:128 + NT * E], ones_bf[:, :], onehot[:, :, :].rearrange("p e t -> p (e t)"), start=True, stop=True).then_inc(counts_done, 1)
                pe.wait_ge(experts_ready, k + 1)
                if k == 0:
                    pe.wait_ge(w2_loaded, 16)

                def turn(q, m, first):
                    s, par = q * 4 + m, m % 2
                    pe.wait_ge(xs_loaded[m], loaded(k, q, m))
                    if first is None or first >= 2:
                        pe.wait_ge(xst_kept, s + (B - 1))
                    pe.transpose(PB[par][:, 0:P], XS[m][:, 0:D], ident[:, :]).then_inc(xs_turned, 1)

                def up(q, m, first):
                    s, par = q * 4 + m, m % 2
                    pe.wait_ge(xst_kept, s + (B + 1))
                    pe.wait_ge(w1_staged, s + (B + 1))
                    if first is None or first >= 2:
                        pe.wait_ge(up_biased, s + (B - 1))
                    for c in range(HC):
                        mm = pe.matmul(PB[2 + par][:, c * P:(c + 1) * P], W1S[par][:, c * P:(c + 1) * P], XST[par][:, :], start=True, stop=True)
                    mm.then_inc(up_done, 1)

                def down(q, m, first, e):
                    s, par = q * 4 + m, m % 2
                    pe.wait_ge(gelu_done, s + (B + 1))
                    if first is None or first >= 2:
                        pe.wait_ge(y_ready, s + (B - 1))
                    for c in range(HC):
                        mm = pe.matmul(PB[4 + par][:, 0:D], HT[par][:, c * P:(c + 1) * P], W2[:, bass.ds(e * HID + c * D, D)], start=(c == 0), stop=(c == HC - 1))
                    mm.then_inc(down_done, 1)

                def steps(q, m, first, last, experts):
                    if last != ST - 1:
                        turn(*after(q, m, 1), None if first is None else first + 1)
                    up(q, m, first)
                    if first != 0:
                        down(*after(q, m, -1), None if first is None else first - 1, experts[m])
                    if last == ST - 1:
                        down(q, m, None, experts[m + 1])
                turn(0, 0, 0)
                tile_pipeline(pe, steps, experts_of(pe, pe_experts))

            def attention():
                pe.wait_ge(attn_w_kept, 2)

                def project(b):
                    for item in range(4 * b, 4 * b + 4):
                        b, z, c = of_item(item)
                        pe.wait_ge(turned_kept, 4 + 2 * b + c + 1)
                        if item >= 4:
                            pe.wait_ge(qk_kept, item - 3)
                        pe.matmul(PB[4 + item % 4], w_attn_t[:, z * D:(z + 1) * D], XT[:, SEQ * b + 512 * c:SEQ * b + 512 * (c + 1)], start=True, stop=True).then_inc(qk_done, 1)
                turn_rows(1, lambda c: project(c // 2) if c % 2 else None)
                for t in range(NT):
                    mm = pe.matmul(PB[t // 4][:, (t % 4) * P:(t % 4 + 1) * P], XT[:, t * P:(t + 1) * P], w_attn_t[:, 2 * D:3 * D], start=True, stop=True)
                    if t % 4 == 3:
                        mm.then_inc(v_done, 1)

                def take_turn(u, g, what):
                    bank = turn_bank[parity[0]]
                    parity[0] = (parity[0] + 1) % TB
                    if not isinstance(u, int) or u >= TB:
                        pe.wait_ge(turn_used, u - (TB - 1))
                    if what[0] == "out":
                        half = what[1]
                        pe.wait_ge(out_kept, (g.n - 1) * 2 + (half + 1))
                        for i in range(4):
                            mm = pe.transpose(bank[:, i * P:(i + 1) * P], out_t[:, 512 * half + i * P:512 * half + (i + 1) * P], ident[:, :])
                    elif what[0] == "turned":
                        c = what[1]
                        for i in range(4):
                            mm = pe.transpose(bank[:, i * P:(i + 1) * P], attn[:, (4 * c + i) * D:(4 * c + i + 1) * D], ident[:, :])
                    elif what[0] == "projected":
                        c = what[1]
                        pe.wait_ge(turn_used, last_turn(("turned", c)))
                        for i in range(4):
                            mm = pe.matmul(bank[:, i * P:(i + 1) * P], attn_t[c][:, i * P:(i + 1) * P], w_proj_t[:, :], start=True, stop=True)
                    elif what[0] == "rows":
                        h, chunk = what[1:]
                        g = g.plus(1)
                        if h == 0 and chunk == 0:
                            pe.wait_ge(qk_loaded[g.slot], g.turn * 96 + 96)
                        for n, (i, key, keys, col) in enumerate(ROW_CHUNKS[chunk]):
                            diag = key + keys == (i + 1) * P
                            last = n == len(ROW_CHUNKS[chunk]) - 1
                            mm = pe.matmul(bank[:, col:col + keys], QK[0:TERMS, g.slot, 0, h, i * P:(i + 1) * P], QK[0:TERMS, g.slot, 1, h, key:key + keys],
                                           start=(n == 0), stop=(last and not diag), skip_group_check=True)
                            if diag:
                                mm = pe.matmul(bank[:, col + keys - P:col + keys], ident_bf[:, :], row_mask[:, :], start=False, stop=last, skip_group_check=True)
                    else:
                        half = what[1]
                        pe.wait_ge(max_parts_ready, (g.n if half and g is not before else g.n + 1) * 2 + (half + 1))
                        mm = pe.transpose(bank.bitcast(BF16)[:, 0:P], max_parts_all[half][:, :], ident_bf[:, :])
                    mm.then_inc(turn_done, 1)

                def scores(g, t, c, first):
                    r = 2 * t + c
                    if t < HG and r % 4 == 0:
                        pe.wait_ge(max_sent[t // 2], g.n * 16 + 16)
                    if r >= 3 or not first:
                        pe.wait_ge(probs_ready, g.n * (2 * CH) + (r - 2))
                    bank = key_bank[r % 3]
                    start = True
                    for h, j, q0 in key_chunk(t):
                        diagonal = q0 + P * j
                        at, end = max(diagonal, 512 * c), min(q0 + SEQ, 512 * (c + 1))
                        if at < end:
                            mm = pe.matmul(bank[:, at - 512 * c:end - 512 * c], QK[0:TERMS + PARTS, g.slot, 1, h, j * P:(j + 1) * P],
                                           QK[0:TERMS + PARTS, g.slot, 0, h, at - q0:end - q0], start=start, stop=False, skip_group_check=True)
                            start = False
                            if at == diagonal:
                                mm = pe.matmul(bank[:, at - 512 * c:at - 512 * c + P], ident_bf[:, :], key_mask[:, :], start=False, stop=True, skip_group_check=True)
                    mm.then_inc(scores_done, 1)

                def piece(g, n, first):
                    j, query, width = PIECES[n]
                    if n == 0:
                        pe.wait_ge(v_staged, g.n + 1)
                    if n in (0, 2) and not first:
                        pe.wait_ge(out_kept, g.n * 2 - 1 + n // 2)
                    pe.wait_ge(probs_ready, g.n * (2 * CH) + 2 * (CH if n >= 16 else 4 * (n // 4) + 4))
                    for h in range(HG):
                        chunk = 16 + h // 2 if n >= 16 else 4 * (n // 4) + h
                        at = query + next(q0 for hh, jj, q0 in key_chunk(chunk) if (hh, jj) == (h, j))
                        mm = pe.matmul(out_acc[32 * h:32 * h + 32, query:query + width], VS[:, g.slot, j, h, :], probs[:, chunk % PROBS, at:at + width],
                                       start=(n in (0, 2)), stop=(n in (12, 17)), skip_group_check=True, tile_position=(0, 32 * h))
                    mm.then_inc(pieces_done, 1)

                parity = [0]
                before = Group(-1, 2, -1)
                pe.wait_ge(v_kept, 4)
                pe.wait_ge(qk_kept, 4 * BATCH)
                for u, what in enumerate(PRO_TURNS):
                    take_turn(u, before, what)

                def steps(g, first, last):
                    u = [0]

                    def turns(place):
                        for what in turns_at(place, first, last):
                            take_turn((len(PRO_TURNS) if first else turns_before(g.n)) + u[0], g, what)
                            u[0] += 1
                    for t in range(CH):
                        for c in range(2):
                            scores(g, t, c, first)
                            turns(3 * t + c)
                        if t >= LAG:
                            piece(g, t - LAG, first)
                        elif not first:
                            piece(g.plus(-1), t - LAG + CH, False)
                        turns(3 * t + 2)
                group_pipeline(pe, steps)
                g = Group(NG - 1, (NG - 1) % 3, (NG - 1) // 3)
                for n in range(CH - LAG, CH):
                    piece(g, n, False)
                for half in range(2):
                    take_turn(turns_before(NG - 1) + len(LAST_TURNS) + half, g.plus(1), ("out", half))
                pe.wait_ge(turn_used, turns_before(NG - 1) + len(LAST_TURNS) + 2)
                for c in (2, 3):
                    for i in range(4):
                        mm = pe.transpose(PB[c][:, i * P:(i + 1) * P], attn[:, (4 * c + i) * D:(4 * c + i + 1) * D], ident[:, :])
                    mm.then_inc(attn_turned, 1)
                for c in (2, 3):
                    pe.wait_ge(attn_kept, c - 1)
                    for i in range(4):
                        mm = pe.matmul(PB[PROJ_BANKS[c]][:, i * P:(i + 1) * P], attn_t[c][:, i * P:(i + 1) * P], w_proj_t[:, :], start=True, stop=True)
                    mm.then_inc(proj_done, 1)

            pe.wait_ge(consts_made, 1)
            pe.wait_ge(small_loaded, 144)
            ffn(0)
            attention()
            ffn(1)

        @block.vector
        def _(dve):
            n = [0]
            dve_experts = [dve.alloc_register(f"dve_expert{j}") for j in range(10)]

            def step(ins):
                n[0] += 1
                ins.then_inc(dve_step, 1)
                dve.wait_ge(dve_step, n[0])

            def refine_rsqrt(r, v, s, a, b):
                step(dve.reciprocal(r, s))
                step(dve.tensor_tensor(a, r, r, ALU.mult))
                step(dve.tensor_tensor(b, a, v, ALU.mult))
                step(dve.tensor_scalar(a, b, -0.5, 1.5, ALU.mult, ALU.add))
                step(dve.tensor_tensor(r, r, a, ALU.mult))

            QT = NT // 4

            def mark(ins):
                n[0] += 1
                ins.then_inc(dve_step, 1)
                return n[0]

            def part_stats(c):
                for t in range(QT * c, QT * (c + 1)):
                    ins = dve.bn_stats(stats[:, t, :], X[:, t, :])
                return mark(ins)

            def variance(h, at):
                dve.wait_ge(dve_step, at)
                for t in range(NT // 2 * h, NT // 2 * (h + 1)):
                    ins = dve.bn_aggr(mean_var[:, t, :], stats[:, t, :])
                step(ins)
                dve.tensor_scalar(var_eps[:, half_tiles(h)], mean_var[:, half_tiles(h), 1], LN_EPS, None, ALU.add).then_inc(norm_var, 1)

            def norm_half(q, h):
                of = half_tiles(h)
                dve.wait_ge(norm_std, 2 * q + h + 1)
                refine_rsqrt(rstd[:, of], var_eps[:, of], std[:, of], newton_a[:, of], newton_b[:, of])
                for t in range(NT // 2 * h, NT // 2 * (h + 1)):
                    dve.tensor_scalar(XR[:, t, 0:D], X[:, t, :], mean_var[:, t, 0:1], rstd[:, t:t + 1], ALU.subtract, ALU.mult).then_inc(norm_rows, 1)

            def norm(q, take, between=lambda: None):
                for c in range(4):
                    take(c)
                    at = part_stats(c)
                    if c == 1:
                        at_half = at
                    if c == 2:
                        variance(0, at_half)
                if q == 0:
                    dve.wait_ge(consts_made, 1)
                norm_half(q, 0)
                between()
                variance(1, at)
                norm_half(q, 1)

            def take_x(c):
                if c % 2 == 0:
                    dve.wait_ge(x_loaded[c // 2], 16)

            def take_stream(c):
                dve.wait_ge(x_back[c], 16)

            def by_tile(a):
                return a.unsqueeze(2).broadcast_to([P, NT, E])

            def route(k):
                dve.wait_ge(consts_made, 2)
                dve.wait_ge(logits_done, k + 1)
                logits = PB[6][:, 0:NT * E].rearrange("p (t e) -> p t e", e=E)
                step(dve.tensor_reduce(gmax[:, :], logits, AX_X, ALU.max))
                dve.tensor_tensor(gt[0][:, :, :], logits, by_tile(gmax[:, :]), ALU.subtract).then_inc(logits_less_max, 1)
                dve.wait_ge(gates_exp, k + 1)
                step(dve.tensor_reduce(gsum[:, :], gt[1][:, :, :], AX_X, ALU.add))
                step(dve.reciprocal(gsum[:, :], gsum[:, :]))
                step(dve.tensor_tensor(gt[2][:, :, :], gt[1][:, :, :], by_tile(gsum[:, :]), ALU.mult))
                step(dve.tensor_reduce(gmax[:, :], gt[2][:, :, :], AX_X, ALU.max))
                dve.tensor_scalar(XR[:, :, HALF_GATE], gmax[:, :], 0.5, None, ALU.mult)
                step(dve.tensor_tensor(gt[3][:, :, :], gt[2][:, :, :], by_tile(gmax[:, :]), ALU.is_ge))
                step(dve.tensor_tensor(gt[2][:, :, :], gt[3][:, :, :], rank_weight[:, :].unsqueeze(1).broadcast_to([P, NT, E]), ALU.mult))
                step(dve.tensor_reduce(gsum[:, :], gt[2][:, :, :], AX_X, ALU.max))
                dve.tensor_tensor(onehot[:, :, :].rearrange("p e t -> p t e"), gt[2][:, :, :], by_tile(gsum[:, :]), ALU.is_equal).then_inc(onehot_ready, 1)
                dve.wait_ge(counts_done, k + 1)
                earlier_less_tile = PB[7][:, 0:NT * E].rearrange("p (e t) -> p e t", e=E)
                by_expert = [a[:, :, :].rearrange("p t e -> p (t e)").rearrange("p (e t) -> p e t", e=E) for a in gt]
                step(dve.tensor_tensor_scan(cum[:, :, :].rearrange("p e t -> p (e t)"), go_on[:, :, :].rearrange("p e t -> p (e t)"),
                                            PB[7][:, 128:128 + NT * E], 0.0, ALU.mult, ALU.add))
                step(dve.tensor_tensor(tile_used[:, :, :], tile_starts[:, :, :], cum[:, :, NT - 1:NT].broadcast_to([P, E, NT]), ALU.is_lt))
                step(dve.tensor_reduce(etiles[:, :], tile_used[:, :, :], AX_X, ALU.add))
                dve.tensor_tensor(by_expert[0], earlier_less_tile, cum[:, :, :], ALU.add)
                step(dve.tensor_tensor_scan(etiles_end[:, :], ones_e[:, :], etiles[:, :], 0.0, ALU.mult, ALU.add))
                step(dve.tensor_tensor(etiles_start[:, :], etiles_end[:, :], etiles[:, :], ALU.subtract))
                step(dve.scalar_tensor_tensor(out=by_expert[1], in0=etiles_start[:, :].unsqueeze(2).broadcast_to([P, E, NT]), scalar=float(P), in1=by_expert[0], op0=ALU.mult, op1=ALU.add))
                step(dve.tensor_tensor(by_expert[2], by_expert[1], onehot[:, :, :], ALU.mult))
                step(dve.tensor_reduce(slot_f[:, :], by_expert[2].rearrange("p e t -> p t e"), AX_X, ALU.add))
                dve.tensor_copy(slot[:, :], slot_f[:, :]).then_inc(slots_ready, 1)
                step(dve.tensor_tensor(tile_ge[:, :, :], slot_tile_no[:, :, :], etiles_end[:, :].unsqueeze(1).broadcast_to([P, ST, E]), ALU.is_ge))
                step(dve.tensor_reduce(tile_expert_f[:, :], tile_ge[:, :, :], AX_X, ALU.add))
                dve.tensor_scalar(tile_expert[:, 1:ST + 1], tile_expert_f[:, :], float(E - 1), None, ALU.min).then_inc(experts_ready, 1)
                dve.wait_ge(experts_ready, k + 1)

            def attention():
                def rest(item):
                    b, z, c = of_item(item)
                    dve.wait_ge(part0_ready, item + 1)
                    if item >= 2:
                        dve.wait_ge(parts_ready, item - 1)
                    dve.tensor_tensor(qk_r[item % 2], qk_f[item % 2], qk_split[z][:, 0, 512 * c:512 * (c + 1)], ALU.subtract).then_inc(rest_ready, 1)

                def middle_part(item):
                    b, z, c = of_item(item)
                    dve.wait_ge(rest_ready, item + 1)
                    dve.tensor_copy(qk_split[z][:, 1, 512 * c:512 * (c + 1)], qk_r[item % 2]).then_inc(part1_ready, 1)

                def last_part(item):
                    b, z, c = of_item(item)
                    dve.wait_ge(part1_ready, item + 1)
                    dve.tensor_tensor(qk_split[z][:, 2, 512 * c:512 * (c + 1)], qk_r[item % 2], qk_split[z][:, 1, 512 * c:512 * (c + 1)], ALU.subtract).then_inc(parts_ready, 1)
                def keep_v():
                    for c in range(4):
                        b = c // 2
                        dve.wait_ge(v_done, c + 1)
                        dve.tensor_tensor(V[:, b * HG:(b + 1) * HG, 4 * (c % 2):4 * (c % 2) + 4, :].rearrange("p g i f -> p i g f"),
                                          PB[c].rearrange("p (i g f) -> p i g f", i=4, g=HG),
                                          b_v[:, :].rearrange("p (g f) -> p g f", g=HG).unsqueeze(1).broadcast_to([P, 4, HG, HG * HD]), ALU.add).then_inc(v_kept, 1)
                for b in range(BATCH):
                    rest(4 * b)
                    for item in range(4 * b, 4 * b + 4):
                        middle_part(item)
                        if item < 4 * b + 3:
                            rest(item + 1)
                        last_part(item)
                    if b == 0:
                        keep_v()


                def maxima(half, u):
                    dve.wait_ge(turn_used, u + 1)
                    dve.tensor_tensor_scan(running_max[half][:, :], restart[:, :], block_max[:, 2 * half:2 * half + 2, :].rearrange("p h b -> p (h b)"),
                                           -LARGE, ALU.min, ALU.max).then_inc(maxima_found, 1)

                def use_turn(u, g, what):
                    bank = turn_bank[parity[0]]
                    parity[0] = (parity[0] + 1) % TB
                    dve.wait_ge(turn_done, u + 1)
                    if what[0] == "out":
                        half = what[1]
                        got = bank.rearrange("p (i h f) -> p i h f", i=4, h=HG)
                        dve.reciprocal(inv_sum[half][:, :, :], got[:, :, :, HD]).then_inc(sums_inverted, 1)
                        dve.wait_ge(sums_inverted, (g.n - 1) * 2 + (half + 1))
                        n = g.n - 1
                        dve.tensor_tensor(attn.rearrange("p (b i f) -> p b i f", b=BATCH, i=KB)[:, bass.ds(n // HG, 1), 4 * half:4 * half + 4, bass.ds(n % HG * (HG * HD), HG * HD)]
                                          .rearrange("p b i (h d) -> p (b i) h d", h=HG), got[:, :, :, 0:HD],
                                          inv_sum[half][:, :, :].unsqueeze(3).broadcast_to([P, 4, HG, HD]), ALU.mult).then_inc(turn_used, 1)
                    elif what[0] == "turned":
                        dve.tensor_copy(attn_t[what[1]], bank).then_inc(turn_used, 1)
                    elif what[0] == "projected":
                        c = what[1]
                        dve.wait_ge(bias_added, 1)
                        dve.tensor_tensor(X[:, QT * c:QT * (c + 1), :], X[:, QT * c:QT * (c + 1), :], bank.rearrange("p (t d) -> p t d", t=QT), ALU.add).then_inc(turn_used, 1)
                    elif what[0] == "rows":
                        h, chunk = what[1:]
                        dve.tensor_reduce(block_max[:, h, 4 * chunk:4 * chunk + 4], bank.rearrange("p (j k) -> p j k", k=P), AX_X, ALU.max).then_inc(turn_used, 1)
                        if h % 2 == 1 and chunk == RC - 1:
                            maxima(h // 2, u)
                    else:
                        half = what[1]
                        if not (isinstance(g.n, int) and g.n + 1 - half == 0):
                            dve.wait_ge(max_sent[half], (g.n + 1 - half) * 16)
                        dve.tensor_copy(max_rows[half][:, :], bank.bitcast(BF16)[0:PARTS * 2 * KB, 0:P]).then_inc(turn_used, 1)

                parity = [0]
                before = Group(-1, 2, -1)
                for u, what in enumerate(PRO_TURNS):
                    use_turn(u, before, what)

                def steps(g, first, last):
                    u = 0
                    for place in range(3 * CH):
                        for what in turns_at(place, first, last):
                            use_turn((len(PRO_TURNS) if first else turns_before(g.n)) + u, g, what)
                            u += 1
                group_pipeline(dve, steps)
                dve.wait_ge(turn_used, last_turn(("projected", 1)))
                for c in range(2):
                    at = part_stats(c)
                variance(0, at)
                for half in range(2):
                    use_turn(turns_before(NG - 1) + len(LAST_TURNS) + half, Group(NG, 0, 0), ("out", half))
                norm_half(2, 0)
                for c in (2, 3):
                    dve.wait_ge(proj_done, c - 1)
                    dve.tensor_tensor(X[:, QT * c:QT * (c + 1), :], X[:, QT * c:QT * (c + 1), :], PB[PROJ_BANKS[c]].rearrange("p (t d) -> p t d", t=QT), ALU.add).then_inc(attended, 1)
                for c in (2, 3):
                    dve.wait_ge(attended, c - 1)
                    at = part_stats(c)
                variance(1, at)
                norm_half(2, 1)

            def keep_weights():
                dve.wait_ge(b1_t_done, 1)
                dve.tensor_copy(b1_cols[:, :], PB[5][:, 0:E * HC])
                dve.wait_ge(attn_w_done, 1)
                dve.tensor_copy(w_attn_t[:, :], PB[4][:, 0:3 * D])
                dve.tensor_copy(b_attn_cols[:, :], PB[5][:, 64:67]).then_inc(attn_w_kept, 1)
                dve.tensor_copy(w_proj_t[:, :], PB[4][:, 3 * D:4 * D]).then_inc(attn_w_kept, 1)

            def ffn(k):
                B = k * ST
                route(k)
                if k == 0:
                    keep_weights()
                    dve.wait_ge(w1_loaded, 16)

                def stage(q, m, first, e):
                    s, par = q * 4 + m, m % 2
                    if first is None or first >= 2:
                        dve.wait_ge(up_done, s + (B - 1))
                    dve.tensor_copy(W1S[par][:, :], W1[:, bass.ds(e * HID, HID)]).then_inc(w1_staged, 1)

                def bias(q, m, first, e):
                    s, par = q * 4 + m, m % 2
                    dve.wait_ge(up_done, s + (B + 1))
                    if first is None or first >= 2:
                        dve.wait_ge(gelu_done, s + (B - 1))
                    dve.tensor_tensor(HB[par][:, :].rearrange("p (c q) -> p c q", c=HC), PB[2 + par][:, :].rearrange("p (c q) -> p c q", c=HC),
                                      b1_cols[:, bass.ds(e * HC, HC)].unsqueeze(2).broadcast_to([P, HC, P]), ALU.add).then_inc(up_biased, 1)

                def finish(q, m, first, e):
                    s, par = q * 4 + m, m % 2
                    dve.wait_ge(down_done, s + (B + 1))
                    if first is None or first >= 2:
                        dve.wait_ge(y_sent[par], sent(k, q, m))
                    dve.tensor_tensor(YB[par][:, :], PB[4 + par][:, 0:D], b2_all[:, bass.ds(e * D, D)], ALU.add).then_inc(y_biased, 1)
                    dve.wait_ge(xg_loaded[m], loaded(k, q, m))
                    dve.wait_ge(y_biased, s + (B + 1))
                    dve.scalar_tensor_tensor(out=YB[par][:, :], in0=YB[par][:, :], scalar=XG[m][:, D:D + 1], in1=XG[m][:, 0:D],
                                             op0=ALU.mult, op1=ALU.add).then_inc(y_ready, 1)

                def steps(q, m, first, last, experts):
                    if last != ST - 1:
                        stage(*after(q, m, 1), None if first is None else first + 1, experts[m + 2])
                    bias(q, m, first, experts[m + 1])
                    if first != 0:
                        finish(*after(q, m, -1), None if first is None else first - 1, experts[m])
                    if last == ST - 1:
                        finish(q, m, None, experts[m + 1])
                stage(0, 0, 0, experts_of(dve, dve_experts)(0, 6)[1])
                tile_pipeline(dve, steps, experts_of(dve, dve_experts))

            def gate_weights():
                dve.wait_ge(small_loaded, 144)
                step(dve.tensor_tensor(wg_sq[:, :], wg_sb[:, :], wg_sb[:, :], ALU.mult))
                step(dve.tensor_reduce(wg_norm[:, 2:3], wg_sq[:, :], AX_X, ALU.add))
                dve.tensor_scalar(wg_norm[:, 0:1], wg_norm[:, 2:3], NORM_EPS * NORM_EPS, None, ALU.max).then_inc(gate_var, 1)
                dve.wait_ge(gate_std, 1)
                refine_rsqrt(wg_norm[:, 3:4], wg_norm[:, 0:1], wg_norm[:, 1:2], wg_norm[:, 4:5], wg_norm[:, 5:6])
                dve.tensor_scalar(wg_unit[:, :], wg_sb[:, :], wg_norm[:, 3:4], None, ALU.mult).then_inc(wgu_t_done, 1)
                dve.wait_ge(gate_w_done, 1)
                dve.tensor_copy(wg_unit_t[:, :], PB[6][0:G, 0:E]).then_inc(wgu_t_done, 1)
                dve.wait_ge(gate_w_done, 2)
                dve.tensor_copy(gate_w[:, :], PB[7][:, 0:E]).then_inc(wgu_t_done, 1)

            dve.memset(tile_expert[:, 0:1], 0)
            dve.memset(tile_expert[:, ST + 1:ST + 3], 0)
            step(dve.memset(ones_e[:, :], 1.0))
            norm(0, take_x, gate_weights)
            ffn(0)
            norm(1, take_stream)
            attention()
            ffn(1)


_INS = ['L0_attn_hidden_states', 'L0_attn_w_attn', 'L0_attn_b_attn', 'L0_attn_w_proj', 'L0_attn_b_proj', 'L0_ffn_wg_red',
        'L0_ffn_wg', 'L0_ffn_w1', 'L0_ffn_b1', 'L0_ffn_w2', 'L0_ffn_b2']


_OUTS = [((2, 1024, 128), 'float32')]


def kernel(**inputs):
    import numpy as _np
    import concourse.bacc as _bacc
    from concourse import mybir as _mybir
    from concourse.bass_utils import run_bass_kernel_spmd as _run

    nc = _bacc.Bacc("TRN2", target_bir_lowering=False, num_devices=1)
    arrays, args = {}, []
    for name in _INS:
        a = _np.ascontiguousarray(inputs[name])
        arrays[f"in_{name}_dram"] = a
        args.append(nc.dram_tensor(f"in_{name}_dram", a.shape, _mybir.dt.from_np(a.dtype), kind="ExternalInput").ap())
    for i, (shape, dtype) in enumerate(_OUTS):
        dt = _mybir.dt.from_np(_np.dtype(dtype))
        args.append(nc.dram_tensor(f"out_{i}_dram", shape, dt, kind="ExternalOutput").ap())
    macaron_kernel(nc, *args)
    r = _run(nc, [arrays], core_ids=[0])
    return r.results[0]["out_0_dram"]
```
